# Optimizing a Trainium2 kernel written in Bass

```python
import numpy as np
import jax
import jax.numpy as jnp

def _softmax(x, axis=-1):
    return jax.nn.softmax(x, axis=axis)

def _gelu(x):
    return jax.nn.gelu(x, approximate=True)

def _silu(x):
    return jax.nn.silu(x)

def _sigmoid(x):
    return jax.nn.sigmoid(x)

def _layernorm(x, axis=-1, eps=1e-05):
    m = jnp.mean(x, axis=axis, keepdims=True)
    v = jnp.var(x, axis=axis, keepdims=True)
    return (x - m) / jnp.sqrt(v + eps)

def _scatter_add(tgt, idx, src, axis=0):
    return tgt.at[idx].add(src)

def _segment_sum(src, seg, n):
    return jax.ops.segment_sum(src, seg, n)
kernel_name = 'mk_recurrent_d1_jaxref_r4_f62941'

def setup_inputs(seed: int=0):
    np.random.seed(seed)
    _w = jnp.asarray

    def _L0_attn_setup():
        import jax, jax.numpy as jnp
        import numpy as np
        import math
        D_INNER, D_STATE, D_CONV, DT_RANK = (512, 16, 4, 128)
        B_SZ, T_LEN = (1, 512)

        def _ssm_forward(x, conv_w, conv_b, xproj_w, dtproj_w, dtproj_b, A_log, D_param):
            B, T, D = x.shape
            N = A_log.shape[1]
            k = conv_w.shape[-1]
            xc = jax.lax.conv_general_dilated(x.transpose(0, 2, 1), conv_w, window_strides=(1,), padding=[(k - 1, 0)], feature_group_count=D, dimension_numbers=('NCH', 'OIH', 'NCH'))
            xc = xc + conv_b[None, :, None]
            x_conv = jax.nn.silu(xc).transpose(0, 2, 1)
            proj = jnp.einsum('btd,pd->btp', x_conv, xproj_w)
            dt_in = proj[..., :DT_RANK]
            B_in = proj[..., DT_RANK:DT_RANK + N]
            C_in = proj[..., DT_RANK + N:]
            delta = jax.nn.softplus(jnp.einsum('btr,dr->btd', dt_in, dtproj_w) + dtproj_b)
            A = -jnp.exp(A_log)
            a = jnp.exp(delta[..., None] * A[None, None])
            b = delta[..., None] * B_in[:, :, None, :] * x_conv[..., None]

            def step(h, ab):
                a_t, b_t = ab
                h = a_t * h + b_t
                return (h, h)
            _, hs = jax.lax.scan(step, jnp.zeros((B, D, N), x.dtype), (a.transpose(1, 0, 2, 3), b.transpose(1, 0, 2, 3)))
            h_all = hs.transpose(1, 0, 2, 3)
            y = jnp.einsum('btdn,btn->btd', h_all, C_in) + x * D_param
            return y
        key = jax.random.key(seed)
        ks = jax.random.split(key, 8)
        x = jax.random.normal(ks[0], (B_SZ, T_LEN, D_INNER), jnp.float32)
        conv_w = jax.random.normal(ks[1], (D_INNER, 1, D_CONV), jnp.float32) * 0.3
        conv_b = jax.random.normal(ks[2], (D_INNER,), jnp.float32) * 0.1
        xproj_w = jax.random.normal(ks[3], (DT_RANK + 2 * D_STATE, D_INNER), jnp.float32) * (1.0 / math.sqrt(D_INNER))
        dtproj_w = jax.random.normal(ks[4], (D_INNER, DT_RANK), jnp.float32) * (1.0 / math.sqrt(DT_RANK))
        dt = jnp.exp(jax.random.uniform(ks[5], (D_INNER,)) * (math.log(0.1) - math.log(0.001)) + math.log(0.001))
        dtproj_b = dt + jnp.log(-jnp.expm1(-dt))
        A_log = jnp.broadcast_to(jnp.log(jnp.arange(1, D_STATE + 1, dtype=jnp.float32))[None, :], (D_INNER, D_STATE))
        D_param = jnp.ones((D_INNER,), jnp.float32)
        return {'x': x, 'conv_w': conv_w, 'conv_b': conv_b, 'xproj_w': xproj_w, 'dtproj_w': dtproj_w, 'dtproj_b': dtproj_b, 'A_log': A_log, 'D_param': D_param}
    _L0_attn_in = _L0_attn_setup()

    def _L0_ffn_setup():
        import jax, jax.numpy as jnp
        import numpy as np
        D_MODEL = 512
        HIDDEN = 4 * D_MODEL
        N_EXPERTS = 8
        TOP_K = 2
        CAP_FACTOR = 1.0
        key = jax.random.key(seed)
        ks = jax.random.split(key, 6)
        x = jax.random.normal(ks[0], (4, 512, D_MODEL), dtype=jnp.float32)
        wg = jax.random.normal(ks[1], (D_MODEL, N_EXPERTS), dtype=jnp.float32) * (1.0 / np.sqrt(D_MODEL))
        fc1_w = jax.random.normal(ks[2], (N_EXPERTS, D_MODEL, HIDDEN), dtype=jnp.float32) * 0.02
        fc1_b = jnp.zeros((N_EXPERTS, HIDDEN), dtype=jnp.float32)
        fc2_w = jax.random.normal(ks[3], (N_EXPERTS, HIDDEN, D_MODEL), dtype=jnp.float32) * 0.02
        fc2_b = jnp.zeros((N_EXPERTS, D_MODEL), dtype=jnp.float32)
        return {'x': x, 'wg': wg, 'fc1_w': fc1_w, 'fc1_b': fc1_b, 'fc2_w': fc2_w, 'fc2_b': fc2_b}
    _L0_ffn_in = _L0_ffn_setup()
    _d = {'L0_attn_x': _L0_attn_in['x'], 'L0_attn_conv_w': _L0_attn_in['conv_w'], 'L0_attn_conv_b': _L0_attn_in['conv_b'], 'L0_attn_xproj_w': _L0_attn_in['xproj_w'], 'L0_attn_dtproj_w': _L0_attn_in['dtproj_w'], 'L0_attn_dtproj_b': _L0_attn_in['dtproj_b'], 'L0_attn_A_log': _L0_attn_in['A_log'], 'L0_attn_D_param': _L0_attn_in['D_param'], 'L0_ffn_wg': _L0_ffn_in['wg'], 'L0_ffn_fc1_w': _L0_ffn_in['fc1_w'], 'L0_ffn_fc1_b': _L0_ffn_in['fc1_b'], 'L0_ffn_fc2_w': _L0_ffn_in['fc2_w'], 'L0_ffn_fc2_b': _L0_ffn_in['fc2_b']}
    _x0 = _d['L0_attn_x']
    _d['L0_attn_x'] = jax.random.normal(jax.random.fold_in(jax.random.key(seed), 1), (2, 2048, 512), dtype=_x0.dtype)
    del _x0
    return _d

def reference(L0_attn_x, L0_attn_conv_w, L0_attn_conv_b, L0_attn_xproj_w, L0_attn_dtproj_w, L0_attn_dtproj_b, L0_attn_A_log, L0_attn_D_param, L0_ffn_wg, L0_ffn_fc1_w, L0_ffn_fc1_b, L0_ffn_fc2_w, L0_ffn_fc2_b):

    def _L0_attn_ref(x, conv_w, conv_b, xproj_w, dtproj_w, dtproj_b, A_log, D_param):
        import jax, jax.numpy as jnp
        import numpy as np
        import math
        D_INNER, D_STATE, D_CONV, DT_RANK = (512, 16, 4, 128)
        B_SZ, T_LEN = (1, 512)

        def _ssm_forward(x, conv_w, conv_b, xproj_w, dtproj_w, dtproj_b, A_log, D_param):
            B, T, D = x.shape
            N = A_log.shape[1]
            k = conv_w.shape[-1]
            xc = jax.lax.conv_general_dilated(x.transpose(0, 2, 1), conv_w, window_strides=(1,), padding=[(k - 1, 0)], feature_group_count=D, dimension_numbers=('NCH', 'OIH', 'NCH'))
            xc = xc + conv_b[None, :, None]
            x_conv = jax.nn.silu(xc).transpose(0, 2, 1)
            proj = jnp.einsum('btd,pd->btp', x_conv, xproj_w)
            dt_in = proj[..., :DT_RANK]
            B_in = proj[..., DT_RANK:DT_RANK + N]
            C_in = proj[..., DT_RANK + N:]
            delta = jax.nn.softplus(jnp.einsum('btr,dr->btd', dt_in, dtproj_w) + dtproj_b)
            A = -jnp.exp(A_log)
            a = jnp.exp(delta[..., None] * A[None, None])
            b = delta[..., None] * B_in[:, :, None, :] * x_conv[..., None]

            def step(h, ab):
                a_t, b_t = ab
                h = a_t * h + b_t
                return (h, h)
            _, hs = jax.lax.scan(step, jnp.zeros((B, D, N), x.dtype), (a.transpose(1, 0, 2, 3), b.transpose(1, 0, 2, 3)))
            h_all = hs.transpose(1, 0, 2, 3)
            y = jnp.einsum('btdn,btn->btd', h_all, C_in) + x * D_param
            return y
        return _ssm_forward(x, conv_w, conv_b, xproj_w, dtproj_w, dtproj_b, A_log, D_param)

    def _L0_ffn_ref(x, wg, fc1_w, fc1_b, fc2_w, fc2_b):
        import jax, jax.numpy as jnp
        import numpy as np
        D_MODEL = 512
        HIDDEN = 4 * D_MODEL
        N_EXPERTS = 8
        TOP_K = 2
        CAP_FACTOR = 1.0
        B, L, D = x.shape
        S = B * L
        E = wg.shape[1]
        K = TOP_K
        C = int(K * S * CAP_FACTOR) // E
        xt = x.reshape(S, D)
        scores = jax.nn.softmax(xt.astype(jnp.float32) @ wg.astype(jnp.float32), axis=-1)
        gate_vals, idx = jax.lax.top_k(scores, K)
        gate_vals = gate_vals / jnp.clip(jnp.sum(gate_vals, axis=-1, keepdims=True), 1e-09)
        counts = jnp.zeros((E,), jnp.int32)
        disp = jnp.zeros((E, C, D), x.dtype)
        pos_safe_l, valid_l = ([], [])
        for s in range(K):
            mask = jax.nn.one_hot(idx[:, s], E, dtype=jnp.int32)
            loc = jnp.cumsum(mask, axis=0) - 1 + counts[None, :]
            pos = jnp.sum(loc * mask, axis=-1)
            counts = counts + jnp.sum(mask, axis=0)
            valid = pos < C
            pos_safe = jnp.where(valid, pos, 0)
            disp = disp.at[idx[:, s], pos_safe].add(xt * valid[:, None].astype(x.dtype))
            pos_safe_l.append(pos_safe)
            valid_l.append(valid)
        h = jax.nn.gelu(jnp.einsum('ecd,edh->ech', disp, fc1_w) + fc1_b[:, None, :], approximate=False)
        eo = jnp.einsum('ech,ehd->ecd', h, fc2_w) + fc2_b[:, None, :]
        y = jnp.zeros((S, D), x.dtype)
        for s in range(K):
            g = (gate_vals[:, s] * valid_l[s].astype(gate_vals.dtype)).astype(x.dtype)
            y = y + g[:, None] * eo[idx[:, s], pos_safe_l[s]]
        return y.reshape(B, L, D)
    x = L0_attn_x
    xn = _layernorm(x, axis=-1)
    s = _L0_attn_ref(xn, L0_attn_conv_w, L0_attn_conv_b, L0_attn_xproj_w, L0_attn_dtproj_w, L0_attn_dtproj_b, L0_attn_A_log, L0_attn_D_param)
    g = _silu(_L0_ffn_ref(xn, L0_ffn_wg, L0_ffn_fc1_w, L0_ffn_fc1_b, L0_ffn_fc2_w, L0_ffn_fc2_b))
    x = x + s * g
    return x

_drawn_inputs = setup_inputs


def setup_inputs(seed=0):
    import zlib

    import numpy as np

    out = dict(_drawn_inputs(seed))
    spreads = {'L0_attn_D_param': (1.0, 0.2), 'L0_ffn_fc1_b': (0.0, 0.1), 'L0_ffn_fc2_b': (0.0, 0.1)}
    factors = {}
    for name, (base, spread) in spreads.items():
        noise = np.random.default_rng([zlib.crc32(name.encode()), seed]).standard_normal(out[name].shape)
        drawn = base * np.exp(spread * noise) if base else spread * noise
        out[name] = jnp.asarray(drawn.astype(out[name].dtype))
    for name, factor in factors.items():
        out[name] = (out[name] * factor).astype(out[name].dtype)
    return out
```

```python
from contextlib import ExitStack

import numpy as np

import concourse.bass as bass
from concourse import mybir

F32 = mybir.dt.float32
F32R = mybir.dt.float32r
I32 = mybir.dt.int32
ALU = mybir.AluOpType
ACT = mybir.ActivationFunctionType
AX = mybir.AxisListType.X
ds = bass.ds

P = 128
B, T, D = 2, 2048, 512
S = B * T
KT = D // P
N = 16
TAPS = 4
R = 128
E, HID = 8, 2048
CAP = 2 * S // E
CH = 512
NCH = S // CH
CPB = T // CH
TPC = CH // P
NT = S // P
TILES = CAP // P
QH = 512
NQ = HID // QH
HT = QH // P
HALO = TAPS - 1
EPS = 1e-5
TRASH = E * CAP
C_TAP, C_CONVB, C_DTB, C_D, C_ALOG = 0, TAPS, TAPS + 1, TAPS + 2, TAPS + 3


class Scratch:

    def __init__(self, nc):
        def dram(name, shape):
            return nc.dram_tensor(name, shape, F32).ap()

        self.xn = dram("xn_rows", (S, D))
        self.slots = dram("slot_table", (E * CAP + 2 * S, 2))
        self.y = dram("moe_rows", (S + CAP, D))
        self.delta = dram("delta_chunks", (NCH, P, KT, CH))
        self.u = dram("u_chunks", (NCH, P, KT, CH))
        self.skip = dram("skip_chunks", (NCH, P, KT, CH))
        self.bc = dram("bc_chunks", (NCH, 2 * N, CH))
        self.s = dram("s_chunks", (NCH + 1, P, KT, CH))


def memory(nc, ctx):
    def sb(name, shape, dt=F32):
        return ctx.enter_context(nc.sbuf_tensor(name, shape, dt))

    def psum(name, shape):
        return ctx.enter_context(nc.psum_tensor(name, shape, F32))

    def sems(prefix, names):
        return {n: ctx.enter_context(nc.semaphore(prefix + n)) for n in names.split()}

    return sb, psum, sems


def apart(eng, sem):
    eng.sem_inc(sem, 1)


def front(nc, a, dr, keep):
    with ExitStack() as ctx:
        sb, psum, sems = memory(nc, ctx)
        ident, tri, ones = sb("f_ident", [P, P]), sb("f_tri", [P, P]), sb("f_ones", [P, P])
        wg = sb("wg_sb", [P, KT, E])
        xprojT = sb("xprojT_sb", [P, KT, R + 2 * N])
        dtprojT = sb("dtprojT_sb", [P, D])
        chan = sb("chan_sb", [P, KT, C_ALOG + N])
        rev, reset = sb("rev_sb", [P, NT, E]), sb("reset_sb", [P, E, NT])
        tokens = sb("tokens_sb", [P, 3, NT])
        mhalf = sb("mhalf_sb", [P, TPC])
        vacant = sb("vacant_sb", [P, E, TILES, 2])
        filled = sb("filled_sb", [P, E, TILES, 2])
        xin = sb("xin_sb", [P, 2, TPC, D])
        xn = sb("xn_sb", [P, 2, TPC, D])
        stats = sb("stats_sb", [P, TPC, 6])
        moments = sb("moments_sb", [P, 2, TPC, 2])
        rstd = sb("rstd_sb", [P, 2, TPC])
        xnT = sb("xnT_sb", [P, NCH + 1, KT, HALO + CH])
        lgT = sb("lgT_sb", [E, CH])
        logits = sb("logits_sb", [P, NT, E])
        zeros = sb("zeros_sb", [P, 512])
        conv = sb("conv_sb", [P, KT, CH])
        xs = sb("xs_sb", [P, 2, KT, CH])
        dtin = sb("dtin_sb", [P, 2, CH])
        bcrows = sb("bcrows_sb", [2 * N, 2, CH])
        za, z = sb("za_sb", [P, KT, CH]), sb("z_sb", [P, KT, CH])
        ln = sb("ln_sb", [P, KT, CH])
        back, skip = sb("back_sb", [P, KT, CH]), sb("skip_sb", [P, KT, CH])
        rt = [sb(f"rt{i}", [P, NT, E]) for i in range(4)]
        mask = [sb(f"mask{s}", [P, NT, E]) for s in range(2)]
        excl = sb("excl_sb", [P, E, NT])
        incl = [sb(f"incl{s}", [P, E, NT]) for s in range(2)]
        tot = sb("tot_sb", [P, E, NT])
        best = [sb(f"best{s}", [P, NT]) for s in range(2)]
        pick = [sb(f"pick{s}", [P, NT]) for s in range(2)]
        c0, c1, c2 = (sb(f"c{i}", [P, NT]) for i in range(3))
        entry = sb("entry_sb", [P, 2, NT, 2])
        place = sb("place_sb", [P, 2, NT], I32)

        pT = psum("pT", [P, 4, CH])
        pX = psum("pX", [P, 2, CH])
        pZ = psum("pZ", [P, 2, CH])

        s_ = sems("f_", """consts x_in0 x_in1 xn_out0 xn_out1 cleared stats moments power normed xT xT_copied
            lgT lgT_copied lg lg_copied route shifted exped masks counted placed defaults scattered table
            indexed zeroed halo tap taps conv_done silu proj dtin bc_rows bc_out0 bc_out1 dt dt_read absz expz
            lnz soft delta u_done skip_done delta_out u_out skip_out neg_a
            pe_at act_at dve_at pool_at sp_at""")

        consts = ((ident, "ident"), (tri, "tri"), (ones, "ones"), (wg, "wg"), (chan, "chan"), (rev, "rev"),
                  (reset, "reset"), (tokens, "tokens"), (xprojT, "xprojT"), (dtprojT, "dtprojT"),
                  (vacant, "vacant"), (mhalf, "mhalf"), (keep["b1"], "fc1_b"))
        block = ctx.enter_context(nc.Block())

        def over_pairs(eng, body):
            with eng.Fori(0, NCH // 2) as i:
                for u in range(2):
                    body(2 * i + u, i, u)

        def skewed(eng, first, second):
            first(0, 0, 0)
            with eng.Fori(0, NCH // 2 - 1) as i:
                first(2 * i + 1, 1, i)
                second(2 * i, 0, i)
                first(2 * i + 2, 0, i + 1)
                second(2 * i + 1, 1, i)
            first(NCH - 1, 1, NCH // 2 - 1)
            second(NCH - 2, 0, NCH // 2 - 1)
            second(NCH - 1, 1, NCH // 2 - 1)

        @block.sync
        def _(sp):
            for name in ("xn_out0", "xn_out1", "delta_out", "u_out", "skip_out"):
                sp.sem_inc(s_[name], 16)
            for dst, src in consts:
                sp.dma_start(dst[:], a[src]).then_inc(s_["consts"], 16)

            def rows(ch, i, u):
                sp.wait_ge(s_["normed"], ch + 1)
                sp.dma_start(xin[:, u], a["x"][ds(ch, 1)].rearrange("o p j d -> p (o j) d")).then_inc(s_[f"x_in{u}"], 16)
                sp.wait_ge(s_["normed"], ch + 3)
                sp.dma_start(dr.xn[ds(ch * CH, CH)].rearrange("(j p) d -> p j d", p=P), xn[:, u]).then_inc(s_[f"xn_out{u}"], 16)

            over_pairs(sp, rows)
            sp.wait_ge(s_["cleared"], 1)
            sp.wait_ge(s_["consts"], 16 * len(consts))
            sp.dma_start(dr.slots[0:TRASH].rearrange("(e p j) k -> p e j k", p=P, j=TILES), vacant[:]).then_inc(s_["defaults"], 16)
            for r in range(0, (S + CAP) // P, 8):
                sp.dma_start(dr.y[r * P:(r + 8) * P].rearrange("(r p) d -> p r d", p=P),
                             zeros[:].unsqueeze(1).to_broadcast([P, 8, D])).then_inc(s_["zeroed"], 16)

            def stores(ch, u, i):
                sp.wait_ge(s_["skip_done"], ch + 1)
                apart(sp, s_["sp_at"])
                sp.dma_start(dr.skip[ds(ch, 1)].rearrange("o p k t -> p (o k) t"), skip[:]).then_inc(s_["skip_out"], 16)
                sp.wait_ge(s_["delta"], ch + 2)
                sp.dma_start(dr.delta[ds(ch, 1)].rearrange("o p k t -> p (o k) t"), ln[:]).then_inc(s_["delta_out"], 16)
                sp.wait_ge(s_["u_done"], ch + 3)
                apart(sp, s_["sp_at"])
                sp.dma_start(dr.u[ds(ch, 1)].rearrange("o p k t -> p (o k) t"), back[:]).then_inc(s_["u_out"], 16)

            skewed(sp, lambda ch, u, i: None, stores)
            sp.wait_ge(s_["scattered"], 16 * 2 * NT)
            sp.dma_start(filled[:], dr.slots[0:TRASH].rearrange("(e p j) k -> p e j k", p=P, j=TILES)).then_inc(s_["table"], 16)
            sp.wait_ge(s_["zeroed"], 16 * ((S + CAP) // P // 8))
            sp.wait_ge(s_["xn_out0"], 16 * NCH // 2 + 16)
            sp.wait_ge(s_["xn_out1"], 16 * NCH // 2 + 16)
            for name in ("delta_out", "u_out", "skip_out"):
                sp.wait_ge(s_[name], 16 * NCH + 16)

        @block.tensor
        def _(pe):
            for name, credits in (("xT", KT + 1), ("lg", 1), ("proj", 1), ("dt", KT + 1)):
                pe.sem_inc(s_[name], credits)
            pe.wait_ge(s_["consts"], 16 * len(consts))

            def turn(ch, i, u):
                pe.wait_ge(s_["normed"], ch + 3)
                for kt in range(KT):
                    pe.wait_ge(s_["xT_copied"], KT * ch + kt + 1)
                    for j in range(TPC):
                        mm = pe.transpose(pT[:, kt, j * P:(j + 1) * P], xn[:, u, j, kt * P:(kt + 1) * P], ident[:])
                    mm.then_inc(s_["xT"], 1)
                pe.wait_ge(s_["xT_copied"], KT * ch + 2 * KT)
                pe.wait_ge(s_["lgT_copied"], ch + 1)
                for kt in range(KT):
                    mm = pe.matmul(pX[0:E, 0, :], wg[:, kt, :], xnT[:, ds(ch, 1), kt, HALO:], start=(kt == 0), stop=(kt == KT - 1))
                mm.then_inc(s_["lgT"], 1)
                pe.wait_ge(s_["lgT_copied"], ch + 2)
                pe.wait_ge(s_["lg_copied"], ch + 1)
                apart(pe, s_["pe_at"])
                for j in range(TPC):
                    mm = pe.transpose(pX[:, 1, j * E:(j + 1) * E], lgT[:, j * P:(j + 1) * P], ident[0:E, 0:E])
                mm.then_inc(s_["lg"], 1)

            over_pairs(pe, turn)

            pe.wait_ge(s_["masks"], 1)
            pe.wait_ge(s_["lg_copied"], NCH + 1)
            for s in range(2):
                for k, w in enumerate((tri, ones)):
                    mm = pe.matmul(pX[:, s, k * NT * E:(k + 1) * NT * E], w[:], mask[s][:].rearrange("p t e -> p (t e)"), start=True, stop=True)
            mm.then_inc(s_["counted"], 1)

            def first(ch, u, i):
                pe.wait_ge(s_["placed"], 1)
                pe.wait_ge(s_["bc_rows"], ch + 1)
                for kt in range(KT):
                    pe.wait_ge(s_["silu"], KT * ch + kt + 2)
                    pe.matmul(pX[:, 0, :], xprojT[:, kt, 0:R], xs[:, u, kt, :], start=(kt == 0), stop=(kt == KT - 1))
                    mm = pe.matmul(pX[0:2 * N, 1, :], xprojT[:, kt, R:R + 2 * N], xs[:, u, kt, :], start=(kt == 0), stop=(kt == KT - 1))
                mm.then_inc(s_["proj"], 1)

            def second(ch, u, i):
                pe.wait_ge(s_["dtin"], ch + 1)
                for kt in range(KT):
                    pe.wait_ge(s_["dt_read"], KT * ch + kt + 1)
                    pe.matmul(pZ[:, kt % 2, :], dtprojT[:, kt * P:(kt + 1) * P], dtin[:, u, :], start=True, stop=True).then_inc(s_["dt"], 1)

            skewed(pe, first, second)

        @block.scalar
        def _(act):
            for name, credits in (("xT_copied", KT), ("lgT_copied", 1), ("lg_copied", 1), ("silu", 1), ("bc_rows", 1),
                                  ("dt_read", 2), ("bc_out0", 16), ("bc_out1", 16)):
                act.sem_inc(s_[name], credits)
            act.wait_ge(s_["consts"], 16 * len(consts))

            def copy_xT(ch, i, u):
                for kt in range(KT):
                    act.wait_ge(s_["xT"], KT * ch + KT + kt + 2)
                    act.activation(xnT[:, ds(ch, 1), kt, HALO:], pT[:, kt, :].unsqueeze(1), ACT.Copy)
                    act.activation(xnT[:, ds(ch + 1, 1), kt, 0:HALO], pT[:, kt, CH - HALO:].unsqueeze(1), ACT.Copy).then_inc(s_["xT_copied"], 1)
                act.wait_ge(s_["lgT"], ch + 1)
                act.wait_ge(s_["lg"], ch + 1)
                act.activation(lgT[:], pX[0:E, 0, :], ACT.Copy).then_inc(s_["lgT_copied"], 1)
                act.wait_ge(s_["lg"], ch + 2)
                act.activation(logits[:, ds(TPC * ch, TPC), :], pX[:, 1, 0:TPC * E].rearrange("p (j e) -> p j e", e=E), ACT.Copy).then_inc(s_["lg_copied"], 1)

            over_pairs(act, copy_xT)

            act.wait_ge(s_["shifted"], 1)
            act.activation(rt[1][:], rt[0][:], ACT.Exp).then_inc(s_["exped"], 1)
            act.activation(keep["neg_a"][:].rearrange("p n k -> p k n"), chan[:, :, C_ALOG:], ACT.Exp).then_inc(s_["neg_a"], 1)

            def first(ch, u, i):
                for kt in range(KT):
                    act.wait_ge(s_["silu"], KT * ch + 1)
                    act.wait_ge(s_["halo"], 1)
                    act.activation(conv[:, kt, :].unsqueeze(1), xnT[:, ds(ch, 1), kt, HALO:], ACT.Identity,
                                   bias=chan[:, kt, C_CONVB:C_CONVB + 1],
                                   scale=chan[:, kt, C_TAP + HALO:C_TAP + HALO + 1]).then_inc(s_["tap"], 1)
                for kt in range(KT):
                    act.wait_ge(s_["conv_done"], KT * ch + kt + 1)
                    act.wait_ge(s_["u_done"], ch + 1)
                    act.wait_ge(s_["proj"], ch + 1)
                    act.activation(xs[:, u, kt, :], conv[:, kt, :], ACT.Silu).then_inc(s_["silu"], 1)
                act.wait_ge(s_["proj"], ch + 2)
                act.wait_ge(s_["dt"], KT * ch + 1)
                act.activation(dtin[:, u, :], pX[:, 0, :], ACT.Copy).then_inc(s_["dtin"], 1)
                act.wait_ge(s_[f"bc_out{u}"], 16 * i + 16)
                act.activation(bcrows[:, u, :], pX[0:2 * N, 1, :], ACT.Copy).then_inc(s_["bc_rows"], 1)
                act.wait_ge(s_["bc_rows"], ch + 2)
                act.dma_start(dr.bc[ds(ch, 1)].rearrange("o n t -> n (o t)"), bcrows[:, u, :]).then_inc(s_[f"bc_out{u}"], 16)

            def second(ch, u, i):
                act.wait_ge(s_["delta"], ch + 1)
                for kt in range(KT):
                    act.wait_ge(s_["dt"], KT * ch + KT + kt + 2)
                    act.activation(z[:, kt, :], pZ[:, kt % 2, :], ACT.Identity, bias=chan[:, kt, C_DTB:C_DTB + 1]).then_inc(s_["dt_read"], 1)
                act.wait_ge(s_["dt_read"], KT * ch + KT + 2)
                act.activation(za[:], z[:], ACT.Abs).then_inc(s_["absz"], 1)
                act.wait_ge(s_["absz"], ch + 1)
                act.activation(za[:], za[:], ACT.Exp, scale=-1.0).then_inc(s_["expz"], 1)
                act.wait_ge(s_["expz"], ch + 1)
                act.wait_ge(s_["delta_out"], 16 * ch + 16)
                act.wait_ge(s_["u_done"], ch + 2)
                act.activation(ln[:], za[:], ACT.Ln, bias=1.0).then_inc(s_["lnz"], 1)

            skewed(act, first, second)
            act.wait_ge(s_["bc_out0"], 16 * NCH // 2 + 16)
            act.wait_ge(s_["bc_out1"], 16 * NCH // 2 + 16)

        @block.gpsimd
        def _(pool):
            pool.sem_inc(s_["u_done"], 2)
            pool.wait_ge(s_["consts"], 16 * len(consts))

            def power(ch, i, u):
                pool.wait_ge(s_["moments"], ch + 1)
                pool.tensor_tensor(rstd[:, u, :], moments[:, u, :, 1], mhalf[:], ALU.pow).then_inc(s_["power"], 1)

            over_pairs(pool, power)

            pool.wait_ge(s_["placed"], 1)
            pool.wait_ge(s_["defaults"], 16)
            for s in range(2):
                for t in range(NT):
                    pool.indirect_dma_start(dr.slots, bass.IndirectOffsetOnAxis(ap=place[:, s, t:t + 1], axis=0),
                                            entry[:, s, t, :], None).then_inc(s_["scattered"], 16)

            def first(ch, u, i):
                pass

            def second(ch, u, i):
                pool.wait_ge(s_["delta"], ch + 2)
                pool.tensor_tensor(back[:], ln[:], xs[:, u], ALU.mult).then_inc(s_["u_done"], 1)

            skewed(pool, first, second)

        @block.vector
        def _(dve):
            dve.sem_inc(s_["normed"], 2)
            dve.sem_inc(s_["delta"], 1)
            dve.memset(zeros[:], 0.0).then_inc(s_["cleared"], 1)
            dve.wait_ge(s_["consts"], 16 * len(consts))

            def norm(ch, i, u):
                dve.wait_ge(s_[f"x_in{u}"], 16 * i + 16)
                for j in range(TPC):
                    dve.bn_stats(stats[:, j, :], xin[:, u, j, :]).then_inc(s_["stats"], 1)
                dve.wait_ge(s_["stats"], (TPC + 2) * ch + TPC)
                apart(dve, s_["dve_at"])
                for j in range(TPC):
                    op = dve.bn_aggr(moments[:, u, j, :], stats[:, j, :])
                op.then_inc(s_["stats"], 1)
                dve.wait_ge(s_["stats"], (TPC + 2) * ch + TPC + 1)
                dve.tensor_scalar(moments[:, u, :, 1], moments[:, u, :, 1], EPS, None, ALU.add).then_inc(s_["stats"], 1)
                dve.wait_ge(s_["stats"], (TPC + 2) * ch + TPC + 2)
                dve.sem_inc(s_["moments"], 1)
                dve.wait_ge(s_["power"], ch + 1)
                dve.wait_ge(s_[f"xn_out{u}"], 16 * i + 16)
                dve.wait_ge(s_["xT"], KT * ch + 1)
                for j in range(TPC):
                    op = dve.tensor_scalar(xn[:, u, j, :], xin[:, u, j, :], moments[:, u, j, 0:1], rstd[:, u, j:j + 1],
                                           ALU.subtract, ALU.mult)
                op.then_inc(s_["normed"], 1)

            over_pairs(dve, norm)

            dve.wait_ge(s_["xT_copied"], KT * NCH + KT)
            for b in range(B):
                op = dve.memset(xnT[:, b * CPB, :, 0:HALO], 0.0)
            op.then_inc(s_["halo"], 1)

            chain = [0]

            def link(op):
                chain[0] += 1
                op.then_inc(s_["route"], 1)
                dve.wait_ge(s_["route"], chain[0])

            def wide(x):
                return x[:].unsqueeze(2).to_broadcast([P, NT, E])

            dve.wait_ge(s_["lg_copied"], NCH + 1)
            link(dve.tensor_reduce(c0[:], logits[:], AX, ALU.max))
            dve.tensor_tensor(rt[0][:], logits[:], wide(c0), ALU.subtract).then_inc(s_["shifted"], 1)
            dve.wait_ge(s_["exped"], 1)
            link(dve.tensor_reduce(c1[:], rt[1][:], AX, ALU.add))
            link(dve.reciprocal(c2[:], c1[:]))
            link(dve.tensor_tensor(rt[2][:], rt[1][:], wide(c2), ALU.mult))
            score = rt[2]
            for s in range(2):
                link(dve.tensor_reduce(best[s][:], score[:], AX, ALU.max))
                link(dve.tensor_tensor(rt[0][:], score[:], wide(best[s]), ALU.is_equal))
                link(dve.tensor_tensor(rt[0][:], rt[0][:], rev[:], ALU.mult))
                link(dve.tensor_reduce(pick[s][:], rt[0][:], AX, ALU.max))
                link(dve.tensor_tensor(mask[s][:], rev[:], wide(pick[s]), ALU.is_equal))
                if s == 0:
                    score = rt[3]
                    link(dve.scalar_tensor_tensor(out=score[:], in0=mask[0][:], scalar=-2.0, in1=rt[2][:], op0=ALU.mult, op1=ALU.add))
            dve.sem_inc(s_["masks"], 1)
            link(dve.tensor_tensor(c0[:], best[0][:], best[1][:], ALU.add))
            link(dve.tensor_scalar(c0[:], c0[:], 1e-9, None, ALU.max))
            link(dve.reciprocal(c1[:], c0[:]))
            for s in range(2):
                link(dve.tensor_tensor(entry[:, s, :, 1], best[s][:], c1[:], ALU.mult))
                link(dve.tensor_copy(entry[:, s, :, 0], tokens[:, 0, :]))
            dve.wait_ge(s_["counted"], 1)
            for s in range(2):
                link(dve.tensor_copy(tot[:], pX[:, s, NT * E:].rearrange("p (t e) -> p e t", e=E)))
                link(dve.tensor_tensor_scan(incl[s][:].rearrange("p e t -> p (e t)"), reset[:].rearrange("p e t -> p (e t)"),
                                            tot[:].rearrange("p e t -> p (e t)"), 0.0, ALU.mult, ALU.add))
                link(dve.tensor_tensor(excl[:], incl[s][:], tot[:], ALU.subtract))
                if s == 1:
                    link(dve.tensor_tensor(excl[:], excl[:], incl[0][:, :, NT - 1:NT].to_broadcast([P, E, NT]), ALU.add))
                link(dve.tensor_tensor(rt[0][:], pX[:, s, 0:NT * E].rearrange("p (t e) -> p t e", e=E), excl[:].rearrange("p e t -> p t e"), ALU.add))
                link(dve.tensor_tensor(rt[0][:], rt[0][:], mask[s][:], ALU.mult))
                link(dve.tensor_reduce(c0[:], rt[0][:], AX, ALU.add))
                link(dve.tensor_scalar(c1[:], pick[s][:], -float(CAP), float(E * CAP - 1), ALU.mult, ALU.add))
                link(dve.tensor_tensor(c1[:], c1[:], c0[:], ALU.add))
                link(dve.tensor_scalar(c2[:], c0[:], float(CAP), None, ALU.is_le))
                link(dve.tensor_tensor(c1[:], c1[:], tokens[:, 1 + s, :], ALU.subtract))
                link(dve.tensor_tensor(c1[:], c1[:], c2[:], ALU.mult))
                link(dve.tensor_tensor(c1[:], c1[:], tokens[:, 1 + s, :], ALU.add))
                link(dve.tensor_copy(place[:, s, :], c1[:]))
            dve.sem_inc(s_["placed"], 1)
            dve.wait_ge(s_["neg_a"], 1)
            link(dve.tensor_scalar(keep["neg_a"][:], keep["neg_a"][:], -1.0, None, ALU.mult))

            def first(ch, u, i):
                dve.wait_ge(s_["tap"], KT * ch + KT)
                for k in range(HALO):
                    for kt in range(KT):
                        if k:
                            dve.wait_ge(s_["taps"], KT * (HALO * ch + k - 1) + kt + 1)
                        op = dve.scalar_tensor_tensor(out=conv[:, kt, :].unsqueeze(1), in0=xnT[:, ds(ch, 1), kt, k:k + CH],
                                                      scalar=chan[:, kt, C_TAP + k:C_TAP + k + 1],
                                                      in1=conv[:, kt, :].unsqueeze(1), op0=ALU.mult, op1=ALU.add)
                        op.then_inc(s_["taps"], 1)
                dve.wait_ge(s_["taps"], KT * HALO * ch + KT * HALO)
                dve.sem_inc(s_["conv_done"], KT)

            def second(ch, u, i):
                dve.wait_ge(s_["skip_out"], 16 * ch + 16)
                for kt in range(KT):
                    op = dve.tensor_scalar(skip[:, kt, :].unsqueeze(1), xnT[:, ds(ch, 1), kt, HALO:], chan[:, kt, C_D:C_D + 1], None, ALU.mult)
                op.then_inc(s_["skip_done"], 1)
                dve.wait_ge(s_["expz"], ch + 1)
                dve.wait_ge(s_["u_out"], 16 * ch + 16)
                dve.tensor_scalar(back[:], za[:], 1.0, -1.0, ALU.add, ALU.add).then_inc(s_["soft"], 1)
                dve.wait_ge(s_["soft"], 3 * ch + 1)
                dve.tensor_tensor(back[:], za[:], back[:], ALU.subtract).then_inc(s_["soft"], 1)
                dve.wait_ge(s_["soft"], 3 * ch + 2)
                dve.scalar_tensor_tensor(out=back[:], in0=z[:], scalar=0.0, in1=back[:], op0=ALU.max, op1=ALU.add).then_inc(s_["soft"], 1)
                dve.wait_ge(s_["soft"], 3 * ch + 3)
                dve.wait_ge(s_["lnz"], ch + 1)
                dve.tensor_tensor(ln[:], ln[:], back[:], ALU.add).then_inc(s_["delta"], 1)

            skewed(dve, first, second)

            dve.wait_ge(s_["table"], 16)
            dve.tensor_copy(keep["add_row"][:, 0], vacant[:, 0, :, 0])
            dve.tensor_copy(keep["add_row"][:, 1:], filled[:, :, :, 0])
            dve.tensor_copy(keep["gate"][:], filled[:, :, :, 1])
            dve.tensor_scalar(keep["row"][:], filled[:, :, :, 0], float(S - 1), None, ALU.min).then_inc(s_["indexed"], 1)
            dve.wait_ge(s_["indexed"], 1)


def main_loop(nc, a, dr, keep):
    with ExitStack() as ctx:
        sb, psum, sems = memory(nc, ctx)
        ident = sb("m_ident", [P, P])
        raw = sb("w_raw", [P, KT * QH])
        w1h, w1l = sb("w1h", [P, KT, QH], F32R), sb("w1l", [P, KT, QH], F32R)
        w2h, w2l = sb("w2h", [P, HT, D], F32R), sb("w2l", [P, HT, D], F32R)
        xTh, xTl = sb("xTh", [P, KT, CAP], F32R), sb("xTl", [P, KT, CAP], F32R)
        hh, hl = sb("hh", [P, 2, HT, 512], F32R), sb("hl", [P, 2, HT, 512], F32R)
        part = sb("part", [P, TILES, D])
        b2 = sb("b2_sb", [P, D])
        got = sb("got", [P, 4, D])
        row_now = sb("row_now", [P, TILES], I32)
        add_now = sb("add_now", [P, TILES], I32)
        u, delta, s_acc = sb("u_sb", [P, KT, CH]), sb("delta_sb", [P, KT, CH]), sb("s_acc", [P, KT, CH])
        abuf = sb("a_sb", [P, 8, 2, CH])
        bbuf = sb("b_sb", [P, 2, 2, CH])
        bc = sb("bc_sb", [P, 2, 2, CH])
        state = sb("state", [P, N, KT])
        ph = psum("ph", [P, 4, 512])
        pacc = psum("pacc", [P, 2, D])
        ptr = psum("ptr", [P, 2, 512])
        s_ = sems("m_", """ident raw_in w_hi w_lo x_got0 x_got1 x_got2 x_got3 x_turned x_hi x_lo l1 gelu h_free l2
            acc_free exp a_free bmul b_free kept scan bc_in0 bc_in1 d_in u_in s_in0 s_in1
            s_out0 s_out1 b2_in staged add_staged added cleared biased pe_at act_at
            dve_at pool_at""")
        block = ctx.enter_context(nc.Block())
        NH = 8 * NQ

        def chunks(eng, body):
            with eng.Fori(0, B) as b:
                with eng.Fori(0, CPB) as c:
                    body(b * CPB + c)

        def quarters(eng, e, quarter):
            quarter(e * NQ, 0, True)
            with eng.Fori(1, NQ) as q:
                quarter(e * NQ + q, q, False)

        @block.sync
        def _(sp):
            sp.dma_start(ident[:], a["ident"]).then_inc(s_["ident"], 16)

            def chunk(e):
                def step_bc(q, k):
                    m = e * N + q * 4 + k
                    sp.wait_ge(s_["a_free"], 2 * m + 6)
                    n = q * 4 + k
                    src = dr.bc[ds(e, 1)].rearrange("o (w n) t -> n (o w) t", w=2)[ds(n, 1)]
                    sp.dma_start(bc[:, k % 2], src.to_broadcast([P, 2, CH])).then_inc(s_[f"bc_in{k % 2}"], 16)

                def weights(it, which):
                    sp.wait_ge(s_["w_lo"], 2 * it + which + 1)
                    sp.wait_ge(s_["w_hi"], 2 * it + which + 1)
                    src = a["w1" if which == 0 else "w2"][ds(it, 1)].rearrange("o p f -> p (o f)")
                    sp.dma_start(raw[:], src).then_inc(s_["raw_in"], 16)

                def store_s(h):
                    sp.wait_ge(s_["b_free"], NH * e + 1 + h)
                    sp.dma_start(dr.s[ds(e, 1), :, 2 * h:2 * h + 2, :].rearrange("o p k t -> p (o k) t"),
                                 s_acc[:, 2 * h:2 * h + 2, :]).then_inc(s_[f"s_out{h}"], 16)

                def load_s(h):
                    sp.wait_ge(s_[f"s_out{h}"], 16 * e + 16)
                    sp.dma_start(s_acc[:, 2 * h:2 * h + 2, :],
                                 dr.skip[ds(e, 1), :, 2 * h:2 * h + 2, :].rearrange("o p k t -> p (o k) t")).then_inc(s_[f"s_in{h}"], 16)

                def quarter(it, q, first):
                    weights(it, 0)
                    step_bc(q, 0)
                    if first:
                        store_s(0)
                        sp.wait_ge(s_["biased"], TILES * e + 1)
                        sp.dma_start(b2[:], a["fc2_b"][ds(e, 1)].to_broadcast([P, D])).then_inc(s_["b2_in"], 16)
                    weights(it, 1)
                    if first:
                        store_s(1)
                        load_s(0)
                        load_s(1)
                    for k in range(1, 4):
                        step_bc(q, k)

                quarters(sp, e, quarter)

            chunks(sp, chunk)
            for h in range(2):
                sp.wait_ge(s_["b_free"], NH * NCH + 1 + h)
                sp.dma_start(dr.s[NCH, :, 2 * h:2 * h + 2, :], s_acc[:, 2 * h:2 * h + 2, :]).then_inc(s_[f"s_out{h}"], 16)
            for h in range(2):
                sp.wait_ge(s_[f"s_out{h}"], 16 * (NCH + 1))

        @block.tensor
        def _(pe):
            for name, credits in (("x_turned", 4), ("l1", 1), ("l2", 1)):
                pe.sem_inc(s_[name], credits)
            pe.wait_ge(s_["ident"], 16)

            def three(out, stat, mov, start, stop):
                (sh, sl), (mh, ml) = stat, mov
                pe.matmul(out, sl, mh, start=start, stop=False)
                pe.matmul(out, sh, ml, start=False, stop=False)
                return pe.matmul(out, sh, mh, start=False, stop=stop)

            def turn(e, t):
                pe.wait_ge(s_[f"x_got{t % 4}"], 16 * (2 * e + t // 4) + 16)
                pe.wait_ge(s_["x_lo"], TILES * e + t + 1)
                for kt in range(KT):
                    mm = pe.transpose(ptr[:, t % 2, kt * P:(kt + 1) * P], got[:, t % 4, kt * P:(kt + 1) * P], ident[:])
                mm.then_inc(s_["x_turned"], 1)

            def chunk(e):
                for t in range(4):
                    turn(e, t)

                def quarter(it, q, first):
                    pe.wait_ge(s_["w_lo"], 2 * it + 2)
                    for g in range(2):
                        if first:
                            pe.wait_ge(s_["x_lo"], TILES * e + 4 * g + 6)
                        for j in range(HT):
                            pe.wait_ge(s_["h_free"], 8 * it + 4 * g + j + 1)
                            for kt in range(KT):
                                w = (w1h[:, kt, j * P:(j + 1) * P], w1l[:, kt, j * P:(j + 1) * P])
                                x = (xTh[:, kt, g * 512:(g + 1) * 512], xTl[:, kt, g * 512:(g + 1) * 512])
                                mm = three(ph[:, j, :], w, x, kt == 0, kt == KT - 1)
                            mm.then_inc(s_["l1"], 1)
                            if first and g == 0:
                                turn(e, 4 + j)
                    pe.wait_ge(s_["w_lo"], 2 * it + 3)
                    for t in range(TILES):
                        g, c = t // 4, (t % 4) * P
                        pe.wait_ge(s_["h_free"], 8 * it + 4 * g + 8)
                        pe.wait_ge(s_["acc_free"], 8 * it + t + 1)
                        for j in range(HT):
                            mm = three(pacc[:, t % 2, :], (hh[:, g, j, c:c + P], hl[:, g, j, c:c + P]),
                                       (w2h[:, j, :], w2l[:, j, :]), j == 0, j == HT - 1)
                        mm.then_inc(s_["l2"], 1)

                quarters(pe, e, quarter)

            chunks(pe, chunk)

        @block.scalar
        def _(act):
            act.sem_inc(s_["w_hi"], 1)
            act.sem_inc(s_["exp"], 1)

            def chunk(e):
                act.wait_ge(s_["exp"], NH * e + 1)
                act.dma_start(delta[:], dr.delta[ds(e, 1)].rearrange("o p k t -> p (o k) t")).then_inc(s_["d_in"], 16)
                act.wait_ge(s_["d_in"], 16 * e + 16)

                def split_w(it, which):
                    hi = w1h if which == 0 else w2h
                    act.wait_ge(s_["raw_in"], 16 * (2 * it + which) + 16)
                    act.wait_ge(s_["l1" if which == 0 else "l2"], 8 * it + 1)
                    act.activation(hi[:].rearrange("p k f -> p (k f)"), raw[:], ACT.Copy).then_inc(s_["w_hi"], 1)

                def split_x(t):
                    act.wait_ge(s_["x_turned"], TILES * e + t + 5)
                    act.activation(xTh[:, :, t * P:(t + 1) * P], ptr[:, t % 2, :].rearrange("p (k s) -> p k s", k=KT), ACT.Copy).then_inc(s_["x_hi"], 1)

                def quarter(it, q, first):
                    for i in range(8):
                        act.wait_ge(s_["a_free"], 8 * it + i + 1)
                        for k in range(2):
                            kt = 2 * (i % 2) + k
                            col = q * 16 + (i // 2) * 4 + kt
                            op = act.activation(abuf[:, i, k, :], delta[:, kt, :], ACT.Exp,
                                                scale=keep["neg_a"][:].rearrange("p n k -> p (n k)")[:, ds(col, 1)])
                        op.then_inc(s_["exp"], 1)
                        if i == 3:
                            split_w(it, 0)
                    if first:
                        for t in range(4):
                            split_x(t)
                    for g in range(2):
                        for j in range(HT):
                            act.wait_ge(s_["l1"], 8 * it + 4 * g + j + 2)
                            apart(act, s_["act_at"])
                            bias = keep["b1"][:, ds(4 * it + j, 1)]
                            act.activation(hh[:, g, j, :], ph[:, j, :], ACT.Gelu, bias=bias)
                            act.activation(ph[:, j, :], ph[:, j, :], ACT.Gelu, bias=bias).then_inc(s_["gelu"], 1)
                            if g == 0 and first:
                                split_x(4 + j)
                            if g == 0 and j == 0:
                                split_w(it, 1)

                quarters(act, e, quarter)

            chunks(act, chunk)

        @block.gpsimd
        def _(pool):
            pool.sem_inc(s_["w_lo"], 1)
            pool.sem_inc(s_["bmul"], 1)

            def chunk(e):
                def gather(t):
                    pool.wait_ge(s_["x_turned"], TILES * e + t + 1)
                    apart(pool, s_["pool_at"])
                    pool.indirect_dma_start(got[:, t % 4, :], None, dr.xn, bass.IndirectOffsetOnAxis(ap=row_now[:, t:t + 1], axis=0)).then_inc(s_[f"x_got{t % 4}"], 16)

                pool.wait_ge(s_["x_turned"], TILES * e + 4)
                pool.tensor_copy(row_now[:], keep["row"][:, ds(e, 1), :].rearrange("p o j -> p (o j)")).then_inc(s_["staged"], 1)
                pool.wait_ge(s_["bmul"], NH * e + 1)
                pool.dma_start(u[:], dr.u[ds(e, 1)].rearrange("o p k t -> p (o k) t")).then_inc(s_["u_in"], 16)
                pool.wait_ge(s_["staged"], e + 1)
                for t in range(4):
                    gather(t)
                pool.wait_ge(s_["u_in"], 16 * e + 16)

                def quarter(it, q, first):
                    def low(which):
                        hi, lo = ((w1h, w1l), (w2h, w2l))[which]
                        pool.wait_ge(s_["w_hi"], 2 * it + which + 2)
                        pool.tensor_tensor(lo[:].rearrange("p k f -> p (k f)"), raw[:], hi[:].rearrange("p k f -> p (k f)").bitcast(F32), ALU.subtract).then_inc(s_["w_lo"], 1)

                    low(0)
                    for i in range(8):
                        m = i // 2
                        if i % 2 == 0:
                            pool.wait_ge(s_[f"bc_in{m % 2}"], 16 * (2 * it + m // 2) + 16)
                        pool.wait_ge(s_["b_free"], 8 * it + i + 1)
                        h = 2 * (i % 2)
                        pool.tensor_tensor(bbuf[:, i % 2], u[:, h:h + 2, :], bc[:, m % 2, 0:1, :].to_broadcast([P, 2, CH]), ALU.mult).then_inc(s_["bmul"], 1)
                        if first and i == 0:
                            for t in range(4, 8):
                                gather(t)
                        if i == 2:
                            low(1)
                        if first and i in (1, 3):
                            if i == 1:
                                pool.wait_ge(s_["acc_free"], 8 * it + 2)
                                pool.tensor_copy(add_now[:], keep["add_row"][:, ds(e, 1), :].rearrange("p o j -> p (o j)")).then_inc(s_["add_staged"], 1)
                                pool.wait_ge(s_["add_staged"], e + 1)
                                apart(pool, s_["pool_at"])
                            for t in range(2 * i - 2, 2 * i + 2):
                                pool.indirect_dma_start(dr.y, bass.IndirectOffsetOnAxis(ap=add_now[:, t:t + 1], axis=0), part[:, t, :], None,
                                                        compute_op=ALU.add).then_inc(s_["added"], 16)

                quarters(pool, e, quarter)

            chunks(pool, chunk)
            pool.wait_ge(s_["acc_free"], 8 * NCH * NQ + 2)
            pool.tensor_copy(add_now[:], keep["add_row"][:, E, :]).then_inc(s_["add_staged"], 1)
            pool.wait_ge(s_["add_staged"], NCH + 1)
            for t in range(TILES):
                pool.indirect_dma_start(dr.y, bass.IndirectOffsetOnAxis(ap=add_now[:, t:t + 1], axis=0), part[:, t, :], None,
                                        compute_op=ALU.add).then_inc(s_["added"], 16)
            pool.wait_ge(s_["added"], 16 * TILES * (NCH + 1))

        @block.vector
        def _(dve):
            dve.memset(part[:], 0.0).then_inc(s_["cleared"], 1)
            dve.memset(s_acc[:], 0.0).then_inc(s_["cleared"], 1)
            dve.wait_ge(s_["cleared"], 2)
            for name, credits in (("x_lo", 2), ("h_free", 4), ("acc_free", 2), ("a_free", 8),
                                  ("b_free", 2), ("biased", 1)):
                dve.sem_inc(s_[name], credits)

            def chunk(e):
                def low_x(t):
                    dve.wait_ge(s_["x_hi"], TILES * e + t + 1)
                    dve.tensor_tensor(xTl[:, :, t * P:(t + 1) * P], ptr[:, t % 2, :].rearrange("p (k s) -> p k s", k=KT),
                                      xTh[:, :, t * P:(t + 1) * P].bitcast(F32), ALU.subtract).then_inc(s_["x_lo"], 1)

                for t in range(4):
                    low_x(t)

                def quarter(it, q, first):
                    for s in range(16):
                        if s < 8:
                            g, j = s // 4, s % 4
                            dve.wait_ge(s_["gelu"], 8 * it + s + 1)
                            dve.tensor_tensor(hl[:, g, j, :], ph[:, j, :], hh[:, g, j, :].bitcast(F32), ALU.subtract).then_inc(s_["h_free"], 1)
                            if first and s < 4:
                                low_x(4 + s)
                        else:
                            t = s - 8
                            gate = keep["gate"][:].rearrange("p e j -> p (e j)")[:, ds(8 * e + t, 1)]
                            if first:
                                if t == 0:
                                    dve.wait_ge(s_["added"], 16 * TILES * e + 16 * TILES)
                                    dve.wait_ge(s_["b2_in"], 16 * e + 16)
                                dve.tensor_scalar(part[:, t, :], b2[:], gate, None, ALU.mult).then_inc(s_["biased"], 1)
                                dve.wait_ge(s_["biased"], TILES * e + t + 2)
                            dve.wait_ge(s_["l2"], 8 * it + t + 2)
                            dve.scalar_tensor_tensor(out=part[:, t, :], in0=pacc[:, t % 2, :], scalar=gate, in1=part[:, t, :],
                                                     op0=ALU.mult, op1=ALU.add).then_inc(s_["acc_free"], 1)
                        i, hs = s // 2, 8 * it + s // 2
                        half, m = i % 2, i // 2
                        kt0 = 2 * half
                        if s % 2 == 0:
                            dve.wait_ge(s_["exp"], hs + 2)
                            dve.wait_ge(s_["bmul"], hs + 2)
                            st = state[:].rearrange("p n k -> p (n k)")
                            for k in range(2):
                                col = q * 16 + m * 4 + kt0 + k
                                op = dve.tensor_tensor_scan(abuf[:, i, k, :], abuf[:, i, k, :], bbuf[:, i % 2, k, :],
                                                            st[:, ds(col, 1)], ALU.mult, ALU.add)
                            op.then_inc(s_["scan"], 1)
                            dve.wait_ge(s_["scan"], hs + 1)
                            apart(dve, s_["dve_at"])
                            dve.tensor_copy(st[:, ds(q * 16 + m * 4 + kt0, 2)].unsqueeze(2), abuf[:, i, :, CH - 1:CH])
                            op = dve.tensor_tensor(bbuf[:, i % 2], abuf[:, i], bc[:, m % 2, 1:2, :].to_broadcast([P, 2, CH]), ALU.mult)
                            op.then_inc(s_["a_free"], 1)
                        else:
                            dve.wait_ge(s_["a_free"], hs + 9)
                            if first and m == 0:
                                dve.wait_ge(s_[f"s_in{half}"], 16 * e + 16)
                            dve.tensor_tensor(s_acc[:, kt0:kt0 + 2, :], s_acc[:, kt0:kt0 + 2, :], bbuf[:, i % 2], ALU.add).then_inc(s_["b_free"], 1)

                quarters(dve, e, quarter)

            with dve.Fori(0, B) as b:
                dve.memset(state[:], 0.0).then_inc(s_["kept"], 1)
                dve.wait_ge(s_["kept"], b + 1)
                apart(dve, s_["dve_at"])
                with dve.Fori(0, CPB) as c:
                    chunk(b * CPB + c)


def tail(nc, a, dr, out):
    with ExitStack() as ctx:
        sb, psum, sems = memory(nc, ctx)
        ident = sb("t_ident", [P, P])
        sT = sb("t_sT", [P, 2, KT, CH])
        y, x = sb("t_y", [P, 2, TPC, D]), sb("t_x", [P, 2, TPC, D])
        g, o = sb("t_g", [P, 2, TPC, D]), sb("t_o", [P, 2, TPC, D])
        ps = psum("t_s", [P, 2, TPC, D])
        s_ = sems("t_", "ident in0 in1 turned silu prod sum out0 out1")
        block = ctx.enter_context(nc.Block())

        def over_pairs(eng, body):
            with eng.Fori(0, NCH // 2) as i:
                for u in range(2):
                    body(2 * i + u, i, u)

        @block.sync
        def _(sp):
            sp.dma_start(ident[:], a["ident"]).then_inc(s_["ident"], 16)

            for u in range(2):
                sp.sem_inc(s_[f"out{u}"], 16)

            def load(ch, u):
                sp.wait_ge(s_["sum"], ch + 1)
                sp.dma_start(sT[:, u], dr.s[ds(ch + 1, 1)].rearrange("o p k t -> p (o k) t")).then_inc(s_[f"in{u}"], 16)
                sp.dma_start(y[:, u], dr.y[ds(ch * CH, CH)].rearrange("(j p) d -> p j d", p=P)).then_inc(s_[f"in{u}"], 16)
                sp.dma_start(x[:, u], a["x"][ds(ch, 1)].rearrange("o p j d -> p (o j) d")).then_inc(s_[f"in{u}"], 16)

            def store(ch, u):
                sp.wait_ge(s_["sum"], ch + 3)
                sp.dma_start(out[ds(ch, 1)].rearrange("o (j p) d -> p (o j) d", p=P), o[:, u]).then_inc(s_[f"out{u}"], 16)

            for u in range(2):
                load(u, u)
            with sp.Fori(1, NCH // 2) as i:
                for u in range(2):
                    store(2 * i + u - 2, u)
                    load(2 * i + u, u)
            for u in range(2):
                store(NCH - 2 + u, u)
            for u in range(2):
                sp.wait_ge(s_[f"out{u}"], 16 * NCH // 2 + 16)

        @block.tensor
        def _(pe):
            pe.wait_ge(s_["ident"], 16)

            def turn(ch, i, u):
                pe.wait_ge(s_[f"in{u}"], 48 * i + 48)
                pe.wait_ge(s_["prod"], ch + 1)
                for j in range(TPC):
                    for kt in range(KT):
                        mm = pe.transpose(ps[:, u, j, kt * P:(kt + 1) * P], sT[:, u, kt, j * P:(j + 1) * P], ident[:])
                mm.then_inc(s_["turned"], 1)

            over_pairs(pe, turn)

        @block.scalar
        def _(act):
            def silu(ch, i, u):
                act.wait_ge(s_[f"in{u}"], 48 * i + 48)
                act.wait_ge(s_["prod"], ch + 1)
                act.activation(g[:, u], y[:, u], ACT.Silu).then_inc(s_["silu"], 1)

            over_pairs(act, silu)

        @block.vector
        def _(dve):
            dve.sem_inc(s_["sum"], 2)
            dve.sem_inc(s_["prod"], 2)

            def combine(ch, i, u):
                dve.wait_ge(s_["silu"], ch + 1)
                dve.wait_ge(s_["turned"], ch + 1)
                dve.wait_ge(s_[f"out{u}"], 16 * i + 16)
                dve.tensor_tensor(o[:, u], ps[:, u], g[:, u], ALU.mult).then_inc(s_["prod"], 1)
                dve.wait_ge(s_["prod"], ch + 3)
                dve.tensor_tensor(o[:, u], o[:, u], x[:, u], ALU.add).then_inc(s_["sum"], 1)

            over_pairs(dve, combine)


def build(nc, a, out):
    dr = Scratch(nc)
    with ExitStack() as ctx:
        sb, _, _ = memory(nc, ctx)
        keep = {
            "b1": sb("b1_keep", [P, E * HID // P]),
            "neg_a": sb("neg_a_keep", [P, N, KT]),
            "row": sb("row_keep", [P, E, TILES], I32),
            "add_row": sb("add_row_keep", [P, E + 1, TILES], I32),
            "gate": sb("gate_keep", [P, E, TILES]),
        }
        front(nc, a, dr, keep)
        main_loop(nc, a, dr, keep)
    tail(nc, a, dr, out)


def lay_out(i):
    def per_channel(x):
        return x.reshape(KT, P, -1).transpose(1, 0, 2)

    chan = np.concatenate([per_channel(x) for x in (
        i["L0_attn_conv_w"].reshape(D, TAPS), i["L0_attn_conv_b"], i["L0_attn_dtproj_b"], i["L0_attn_D_param"], i["L0_attn_A_log"])], axis=2)
    w1 = i["L0_ffn_fc1_w"].reshape(E, KT, P, NQ, QH).transpose(0, 3, 2, 1, 4)
    w2 = i["L0_ffn_fc2_w"].reshape(E, NQ, HT, P, D).transpose(0, 1, 3, 2, 4)
    return {
        "x": i["L0_attn_x"].reshape(NCH, TPC, P, D).transpose(0, 2, 1, 3),
        "chan": chan,
        "xprojT": i["L0_attn_xproj_w"].T.reshape(KT, P, R + 2 * N).transpose(1, 0, 2),
        "dtprojT": i["L0_attn_dtproj_w"].T,
        "wg": i["L0_ffn_wg"].reshape(KT, P, E).transpose(1, 0, 2),
        "w1": w1.reshape(E * NQ, P, KT * QH),
        "w2": w2.reshape(E * NQ, P, HT * D),
        "fc1_b": i["L0_ffn_fc1_b"].reshape(E * HID // P, P).T,
        "fc2_b": i["L0_ffn_fc2_b"],
    }


def constants():
    f = np.float32
    token = (np.arange(NT)[None, :] * P + np.arange(P)[:, None]).astype(f)
    slot = np.arange(CAP).reshape(P, TILES)
    vacant = np.zeros((P, E, TILES, 2), f)
    vacant[..., 0] = (S + slot)[:, None, :]
    reset = np.ones((P, E, NT), f)
    reset[:, :, 0] = 0
    return {
        "ident": np.eye(P, dtype=f),
        "tri": np.triu(np.ones((P, P), f)),
        "ones": np.ones((P, P), f),
        "rev": np.broadcast_to((E - np.arange(E)).astype(f), (P, NT, E)),
        "reset": reset,
        "tokens": np.stack([token, TRASH + token, TRASH + S + token], axis=1),
        "mhalf": np.full((P, TPC), -0.5, f),
        "vacant": vacant,
    }


def kernel(**inputs):
    import concourse.bacc as bacc
    from concourse.bass_utils import run_bass_kernel_spmd

    nc = bacc.Bacc("TRN2", target_bir_lowering=False, num_devices=1)
    given = lay_out({k: np.asarray(v) for k, v in inputs.items()})
    given.update(constants())
    arrays, aps = {}, {}
    for name, value in given.items():
        value = np.ascontiguousarray(value)
        arrays[f"in_{name}"] = value
        aps[name] = nc.dram_tensor(f"in_{name}", value.shape, mybir.dt.from_np(value.dtype), kind="ExternalInput").ap()
    out = nc.dram_tensor("out", (NCH, CH, D), F32, kind="ExternalOutput").ap()
    build(nc, aps, out)
    r = run_bass_kernel_spmd(nc, [arrays], core_ids=[0])
    return np.asarray(r.results[0]["out"]).reshape(B, T, D)
```

```python
from contextlib import ExitStack

import numpy as np

import concourse.bass as bass
from concourse import mybir

F32 = mybir.dt.float32
F32R = mybir.dt.float32r
I32 = mybir.dt.int32
ALU = mybir.AluOpType
ACT = mybir.ActivationFunctionType
AX = mybir.AxisListType.X
ds = bass.ds

P = 128
B, T, D = 2, 2048, 512
S = B * T
KT = D // P
N = 16
TAPS = 4
R = 128
E, HID = 8, 2048
CAP = 2 * S // E
CH = 512
NCH = S // CH
CPB = T // CH
TPC = CH // P
NT = S // P
TILES = CAP // P
QH = 512
NQ = HID // QH
HT = QH // P
HALO = TAPS - 1
EPS = 1e-5
TRASH = E * CAP
C_TAP, C_CONVB, C_DTB, C_D, C_ALOG = 0, TAPS, TAPS + 1, TAPS + 2, TAPS + 3


class Scratch:

    def __init__(self, nc):
        def dram(name, shape):
            return nc.dram_tensor(name, shape, F32).ap()

        self.xn = dram("xn_rows", (S, D))
        self.slots = dram("slot_table", (E * CAP + 2 * S, 2))
        self.y = dram("moe_rows", (S + CAP, D))
        self.delta = dram("delta_chunks", (NCH, P, KT, CH))
        self.u = dram("u_chunks", (NCH, P, KT, CH))
        self.bc = dram("bc_chunks", (NCH, 2 * N, CH))
        self.s = dram("s_chunks", (NCH + 1, P, KT, CH))


def memory(nc, ctx):
    def sb(name, shape, dt=F32):
        return ctx.enter_context(nc.sbuf_tensor(name, shape, dt))

    def psum(name, shape):
        return ctx.enter_context(nc.psum_tensor(name, shape, F32))

    def sems(prefix, names):
        return {n: ctx.enter_context(nc.semaphore(prefix + n)) for n in names.split()}

    return sb, psum, sems


def apart(eng, sem):
    eng.sem_inc(sem, 1)


def front(nc, a, dr, keep):
    with ExitStack() as ctx:
        sb, psum, sems = memory(nc, ctx)
        ident, tri, ones = sb("f_ident", [P, P]), sb("f_tri", [P, P]), sb("f_ones", [P, P])
        wg = sb("wg_sb", [P, KT, E])
        xprojT = sb("xprojT_sb", [P, KT, R + 2 * N])
        dtprojT = sb("dtprojT_sb", [P, D])
        chan = sb("chan_sb", [P, KT, C_ALOG + N])
        rev, reset = sb("rev_sb", [P, NT, E]), sb("reset_sb", [P, E, NT])
        tokens = sb("tokens_sb", [P, 3, NT])
        mhalf = sb("mhalf_sb", [P, TPC])
        vacant = sb("vacant_sb", [P, E, TILES, 2])
        filled = sb("filled_sb", [P, E, TILES, 2])
        xin = sb("xin_sb", [P, 2, TPC, D])
        xn = sb("xn_sb", [P, 2, TPC, D])
        stats = sb("stats_sb", [P, TPC, 6])
        moments = sb("moments_sb", [P, 2, TPC, 2])
        rstd = sb("rstd_sb", [P, 2, TPC])
        xnT = sb("xnT_sb", [P, NCH + 1, KT, HALO + CH])
        lgT = sb("lgT_sb", [E, CH])
        logits = sb("logits_sb", [P, NT, E])
        zeros = sb("zeros_sb", [P, 512])
        conv = sb("conv_sb", [P, KT, CH])
        dtin = sb("dtin_sb", [P, CH])
        bcrows = sb("bcrows_sb", [2 * N, CH])
        za, z = sb("za_sb", [P, KT, CH]), sb("z_sb", [P, KT, CH])
        ln = sb("ln_sb", [P, KT, CH])
        back, skip = sb("back_sb", [P, KT, CH]), sb("skip_sb", [P, KT, CH])
        u_now = sb("u_now_sb", [P, KT, CH])
        rt = [sb(f"rt{i}", [P, NT, E]) for i in range(4)]
        mask = [sb(f"mask{s}", [P, NT, E]) for s in range(2)]
        excl = sb("excl_sb", [P, E, NT])
        incl = [sb(f"incl{s}", [P, E, NT]) for s in range(2)]
        tot = sb("tot_sb", [P, E, NT])
        best = [sb(f"best{s}", [P, NT]) for s in range(2)]
        pick = [sb(f"pick{s}", [P, NT]) for s in range(2)]
        c0, c1, c2 = (sb(f"c{i}", [P, NT]) for i in range(3))
        entry = sb("entry_sb", [P, 2, NT, 2])
        place = sb("place_sb", [P, 2, NT], I32)

        pT = psum("pT", [P, 4, CH])
        pX = psum("pX", [P, 2, CH])
        pC = psum("pC", [P, 2, CH])

        s_ = sems("f_", """early consts x_in0 x_in1 xn_out0 xn_out1 cleared stats moments power normed xT xT_copied
            lgT lgT_copied lg lg_copied route shifted exped masks counted placed defaults scattered table
            indexed zeroed halo taps silu proj dtin bc_rows bc_out dt dt_read absz expz
            lnz rounded dropped dropped_dve soft delta u_done skip_done delta_out u_out skip_out neg_a
            pe_at act_at dve_at sp_at""")

        early = ((ident, "ident"), (wg, "wg"), (mhalf, "mhalf"))
        consts = ((tri, "tri"), (ones, "ones"), (chan, "chan"), (rev, "rev"),
                  (reset, "reset"), (tokens, "tokens"), (xprojT, "xprojT"), (dtprojT, "dtprojT"),
                  (vacant, "vacant"), (keep["b1"], "fc1_b"))
        HALVES = (slice(0, KT // 2), slice(KT // 2, KT))
        FIRST_SCATTERS, NEXT_SCATTERS = 20, 8
        AHEAD = 2
        block = ctx.enter_context(nc.Block())

        def over_pairs(eng, body):
            with eng.Fori(0, NCH // 2) as i:
                for u in range(2):
                    body(2 * i + u, i, u)

        @block.sync
        def _(sp):
            for name in ("xn_out0", "xn_out1", "delta_out", "u_out", "skip_out"):
                sp.sem_inc(s_[name], 16)

            def load(ch, u):
                sp.wait_ge(s_["normed"], ch + 1)
                sp.dma_start(xin[:, u], a["x"][ds(ch, 1)].rearrange("o p j d -> p (o j) d")).then_inc(s_[f"x_in{u}"], 16)

            def store(ch, u):
                sp.wait_ge(s_["normed"], ch + 3)
                sp.dma_start(dr.xn[ds(ch * CH, CH)].rearrange("(j p) d -> p j d", p=P), xn[:, u]).then_inc(s_[f"xn_out{u}"], 16)

            for u in range(2):
                load(u, u)
            for name, group in (("early", early), ("consts", consts)):
                for dst, src in group:
                    sp.dma_start(dst[:], a[src]).then_inc(s_[name], 16)
            with sp.Fori(1, NCH // 2) as i:
                for u in range(2):
                    load(2 * i + u, u)
                    store(2 * i + u - 2, u)
            for u in range(2):
                store(NCH - 2 + u, u)
            sp.wait_ge(s_["cleared"], 1)
            sp.dma_start(dr.s[0], zeros[:].unsqueeze(1).to_broadcast([P, KT, CH])).then_inc(s_["zeroed"], 16)
            sp.wait_ge(s_["consts"], 16 * len(consts))
            sp.dma_start(dr.slots[0:TRASH].rearrange("(e p j) k -> p e j k", p=P, j=TILES), vacant[:]).then_inc(s_["defaults"], 16)
            for r in range(0, (S + CAP) // P, 8):
                sp.dma_start(dr.y[r * P:(r + 8) * P].rearrange("(r p) d -> p r d", p=P),
                             zeros[:].unsqueeze(1).to_broadcast([P, 8, D])).then_inc(s_["zeroed"], 16)

            def store_skip(ch):
                sp.wait_ge(s_["skip_done"], ch + 1)
                apart(sp, s_["sp_at"])
                sp.dma_start(dr.s[ds(ch + 1, 1)].rearrange("o p k t -> p (o k) t"), skip[:]).then_inc(s_["skip_out"], 16)

            def store_du(ch):
                sp.wait_ge(s_["delta"], 2 * ch + 3)
                apart(sp, s_["sp_at"])
                sp.dma_start(dr.delta[ds(ch, 1)].rearrange("o p k t -> p (o k) t"), ln[:]).then_inc(s_["delta_out"], 16)
                sp.wait_ge(s_["u_done"], 2 * ch + 3)
                apart(sp, s_["sp_at"])
                sp.dma_start(dr.u[ds(ch, 1)].rearrange("o p k t -> p (o k) t"), u_now[:]).then_inc(s_["u_out"], 16)

            for ch in range(AHEAD):
                store_skip(ch)
            with sp.Fori(0, NCH - AHEAD) as ch:
                store_skip(ch + AHEAD)
                store_du(ch)
            sp.wait_ge(s_["scattered"], 16 * 2 * NT)
            sp.dma_start(filled[:], dr.slots[0:TRASH].rearrange("(e p j) k -> p e j k", p=P, j=TILES)).then_inc(s_["table"], 16)
            for ch in range(NCH - AHEAD, NCH):
                store_du(ch)
            sp.wait_ge(s_["zeroed"], 16 * ((S + CAP) // P // 8 + 1))
            sp.wait_ge(s_["xn_out0"], 16 * NCH // 2 + 16)
            sp.wait_ge(s_["xn_out1"], 16 * NCH // 2 + 16)
            for name in ("delta_out", "u_out", "skip_out"):
                sp.wait_ge(s_[name], 16 * NCH + 16)

        @block.tensor
        def _(pe):
            for name, credits in (("xT", KT + 1), ("lg", 1), ("proj", 1), ("dt", 1)):
                pe.sem_inc(s_[name], credits)
            pe.wait_ge(s_["early"], 16 * len(early))

            def turn(ch, u, i):
                pe.wait_ge(s_["normed"], ch + 3)
                for kt in range(KT):
                    pe.wait_ge(s_["xT_copied"], KT * ch + kt + 1)
                    for j in range(TPC):
                        mm = pe.transpose(pT[:, kt, j * P:(j + 1) * P], xn[:, u, j, kt * P:(kt + 1) * P], ident[:])
                    mm.then_inc(s_["xT"], 1)

            def logits_T(ch):
                pe.wait_ge(s_["xT_copied"], KT * ch + 2 * KT)
                pe.wait_ge(s_["lgT_copied"], ch + 1)
                for kt in range(KT):
                    mm = pe.matmul(pX[0:E, 0, :], wg[:, kt, :], xnT[:, ds(ch, 1), kt, HALO:], start=(kt == 0), stop=(kt == KT - 1))
                mm.then_inc(s_["lgT"], 1)

            def turn_logits(ch):
                pe.wait_ge(s_["lgT_copied"], ch + 2)
                pe.wait_ge(s_["lg_copied"], ch + 1)
                apart(pe, s_["pe_at"])
                for j in range(TPC):
                    mm = pe.transpose(pX[:, 1, j * E:(j + 1) * E], lgT[:, j * P:(j + 1) * P], ident[0:E, 0:E])
                mm.then_inc(s_["lg"], 1)

            turn(0, 0, 0)
            with pe.Fori(0, NCH // 2 - 1) as i:
                for u in range(2):
                    logits_T(2 * i + u)
                    turn(2 * i + u + 1, 1 - u, i)
                    turn_logits(2 * i + u)
            logits_T(NCH - 2)
            turn(NCH - 1, 1, 0)
            turn_logits(NCH - 2)
            logits_T(NCH - 1)
            turn_logits(NCH - 1)

            pe.wait_ge(s_["consts"], 16 * len(consts))
            pe.wait_ge(s_["masks"], 1)
            pe.wait_ge(s_["lg_copied"], NCH + 1)
            for s in range(2):
                for k, w in enumerate((tri, ones)):
                    mm = pe.matmul(pC[:, s, k * NT * E:(k + 1) * NT * E], w[:], mask[s][:].rearrange("p t e -> p (t e)"), start=True, stop=True)
            mm.then_inc(s_["counted"], 1)

            def project(ch):
                pe.wait_ge(s_["bc_rows"], ch + 1)
                for kt in range(KT):
                    pe.wait_ge(s_["silu"], KT * ch + kt + 2)
                    xs = xnT[:, ds(ch, 1), kt, HALO:]
                    pe.matmul(pX[:, 0, :], xprojT[:, kt, 0:R], xs, start=(kt == 0), stop=(kt == KT - 1))
                    mm = pe.matmul(pX[0:2 * N, 1, :], xprojT[:, kt, R:R + 2 * N], xs, start=(kt == 0), stop=(kt == KT - 1))
                mm.then_inc(s_["proj"], 1)

            def widen_dt(ch):
                pe.wait_ge(s_["dtin"], ch + 1)
                for kt in range(KT):
                    pe.wait_ge(s_["dt_read"], KT * ch + kt + 1)
                    pe.matmul(pT[:, kt, :], dtprojT[:, kt * P:(kt + 1) * P], dtin[:], start=True, stop=True).then_inc(s_["dt"], 1)

            with pe.Fori(0, NCH) as ch:
                project(ch)
                widen_dt(ch)

        @block.scalar
        def _(act):
            for name, credits in (("xT_copied", KT), ("lgT_copied", 1), ("lg_copied", 1), ("silu", 1), ("bc_rows", 1),
                                  ("dt_read", KT), ("bc_out", 16)):
                act.sem_inc(s_[name], credits)

            def copy_xT(ch):
                for kt in range(KT):
                    act.wait_ge(s_["xT"], KT * ch + KT + kt + 2)
                    act.activation(xnT[:, ds(ch, 1), kt, HALO:], pT[:, kt, :].unsqueeze(1), ACT.Copy)
                    act.activation(xnT[:, ds(ch + 1, 1), kt, 0:HALO], pT[:, kt, CH - HALO:].unsqueeze(1), ACT.Copy).then_inc(s_["xT_copied"], 1)

            def copy_lgT(ch):
                act.wait_ge(s_["lgT"], ch + 1)
                act.wait_ge(s_["lg"], ch + 1)
                act.activation(lgT[:], pX[0:E, 0, :], ACT.Copy).then_inc(s_["lgT_copied"], 1)

            def copy_lg(ch):
                act.wait_ge(s_["lg"], ch + 2)
                act.activation(logits[:, ds(TPC * ch, TPC), :], pX[:, 1, 0:TPC * E].rearrange("p (j e) -> p j e", e=E), ACT.Copy).then_inc(s_["lg_copied"], 1)

            copy_xT(0)
            with act.Fori(0, NCH - 1) as ch:
                copy_lgT(ch)
                copy_xT(ch + 1)
                copy_lg(ch)
            copy_lgT(NCH - 1)
            copy_lg(NCH - 1)

            act.wait_ge(s_["consts"], 16 * len(consts))
            act.wait_ge(s_["shifted"], 1)
            act.activation(rt[1][:], rt[0][:], ACT.Exp).then_inc(s_["exped"], 1)
            act.activation(keep["neg_a"][:].rearrange("p n k -> p k n"), chan[:, :, C_ALOG:], ACT.Exp).then_inc(s_["neg_a"], 1)

            def silu(ch):
                act.wait_ge(s_["skip_done"], ch + 1)
                for kt in range(KT):
                    act.wait_ge(s_["taps"], KT * (TAPS * ch + HALO) + kt + 1)
                    apart(act, s_["act_at"])
                    act.activation(xnT[:, ds(ch, 1), kt, HALO:], conv[:, kt, :].unsqueeze(1), ACT.Silu).then_inc(s_["silu"], 1)

            def copy_projection(ch):
                act.wait_ge(s_["proj"], ch + 2)
                act.wait_ge(s_["dt"], KT * ch + 1)
                act.activation(dtin[:], pX[:, 0, :], ACT.Copy).then_inc(s_["dtin"], 1)
                act.wait_ge(s_["bc_out"], 16 * ch + 16)
                act.activation(bcrows[:], pX[0:2 * N, 1, :], ACT.Copy).then_inc(s_["bc_rows"], 1)

            def softplus(ch):
                act.wait_ge(s_["soft"], 2 * ch + 2)
                for h in HALVES:
                    for kt in range(h.start, h.stop):
                        act.wait_ge(s_["dt"], KT * ch + kt + 2)
                        act.activation(z[:, kt, :], pT[:, kt, :], ACT.Identity, bias=chan[:, kt, C_DTB:C_DTB + 1]).then_inc(s_["dt_read"], 1)
                    act.wait_ge(s_["dt_read"], KT * ch + KT + h.stop)
                    act.activation(za[:, h], z[:, h], ACT.Abs).then_inc(s_["absz"], 1)
                    act.wait_ge(s_["absz"], 2 * ch + h.stop // 2)
                    act.activation(za[:, h], za[:, h], ACT.Exp, scale=-1.0).then_inc(s_["expz"], 1)
                act.wait_ge(s_["expz"], 2 * ch + 2)
                act.wait_ge(s_["delta_out"], 16 * ch + 16)
                act.wait_ge(s_["u_done"], 2 * ch + 1)
                for h in HALVES:
                    act.activation(ln[:, h], za[:, h], ACT.Ln, bias=1.0).then_inc(s_["lnz"], 1)

            def store_bc(ch):
                act.wait_ge(s_["bc_rows"], ch + 2)
                act.dma_start(dr.bc[ds(ch, 1)].rearrange("o n t -> n (o t)"), bcrows[:]).then_inc(s_["bc_out"], 16)

            silu(0)
            with act.Fori(0, NCH - 1) as ch:
                copy_projection(ch)
                silu(ch + 1)
                store_bc(ch)
                softplus(ch)
            copy_projection(NCH - 1)
            store_bc(NCH - 1)
            softplus(NCH - 1)
            act.wait_ge(s_["bc_out"], 16 * NCH + 16)

        @block.gpsimd
        def _(pool):
            pool.sem_inc(s_["u_done"], 1)
            pool.wait_ge(s_["early"], 16 * len(early))

            def power(ch, i, u):
                pool.wait_ge(s_["moments"], ch + 1)
                pool.tensor_tensor(rstd[:, u, :], moments[:, u, :, 1], mhalf[:], ALU.pow).then_inc(s_["power"], 1)

            over_pairs(pool, power)

            pool.wait_ge(s_["placed"], 1)
            pool.wait_ge(s_["defaults"], 16)
            choices = [(s, t) for s in range(2) for t in range(NT)]
            begin = 0
            for ch in range(NCH):
                end = min(len(choices), FIRST_SCATTERS + ch * NEXT_SCATTERS)
                for s, t in choices[begin:end]:
                    pool.indirect_dma_start(dr.slots, bass.IndirectOffsetOnAxis(ap=place[:, s, t:t + 1], axis=0),
                                            entry[:, s, t, :], None).then_inc(s_["scattered"], 16)
                begin = end
                pool.wait_ge(s_["rounded"], 2 * ch + 1)
                pool.tensor_tensor(back[:, HALVES[0]], za[:, HALVES[0]], back[:, HALVES[0]], ALU.subtract).then_inc(s_["dropped"], 1)
                pool.wait_ge(s_["u_out"], 16 * ch + 16)
                for n, h in enumerate(HALVES):
                    pool.wait_ge(s_["delta"], 2 * ch + n + 2)
                    pool.tensor_tensor(u_now[:, h], ln[:, h], xnT[:, ch, h, HALO:], ALU.mult).then_inc(s_["u_done"], 1)

        @block.vector
        def _(dve):
            dve.sem_inc(s_["normed"], 2)
            dve.sem_inc(s_["soft"], 2)
            dve.sem_inc(s_["delta"], 1)
            dve.memset(zeros[:], 0.0).then_inc(s_["cleared"], 1)

            def measure(ch, u, i):
                dve.wait_ge(s_[f"x_in{u}"], 16 * i + 16)
                for j in range(TPC):
                    dve.bn_stats(stats[:, j, :], xin[:, u, j, :]).then_inc(s_["stats"], 1)
                dve.wait_ge(s_["stats"], (TPC + 2) * ch + TPC)
                apart(dve, s_["dve_at"])
                for j in range(TPC):
                    op = dve.bn_aggr(moments[:, u, j, :], stats[:, j, :])
                op.then_inc(s_["stats"], 1)
                dve.wait_ge(s_["stats"], (TPC + 2) * ch + TPC + 1)
                dve.tensor_scalar(moments[:, u, :, 1], moments[:, u, :, 1], EPS, None, ALU.add).then_inc(s_["stats"], 1)
                dve.wait_ge(s_["stats"], (TPC + 2) * ch + TPC + 2)
                dve.sem_inc(s_["moments"], 1)

            def norm(ch, u, i):
                dve.wait_ge(s_["power"], ch + 1)
                dve.wait_ge(s_[f"xn_out{u}"], 16 * i + 16)
                dve.wait_ge(s_["xT"], KT * ch + 1)
                for j in range(TPC):
                    op = dve.tensor_scalar(xn[:, u, j, :], xin[:, u, j, :], moments[:, u, j, 0:1], rstd[:, u, j:j + 1],
                                           ALU.subtract, ALU.mult)
                op.then_inc(s_["normed"], 1)

            def normalise(ch, i, u):
                measure(ch, u, i)
                norm(ch, u, i)

            over_pairs(dve, normalise)

            dve.wait_ge(s_["consts"], 16 * len(consts))
            dve.wait_ge(s_["xT_copied"], KT * NCH + KT)
            for b in range(B):
                op = dve.memset(xnT[:, b * CPB, :, 0:HALO], 0.0)
            op.then_inc(s_["halo"], 1)

            def convolve(ch):
                dve.wait_ge(s_["silu"], KT * ch + 1)
                for k in range(TAPS):
                    for kt in range(KT):
                        x = xnT[:, ds(ch, 1), kt, HALO - k:HALO - k + CH]
                        c = conv[:, kt, :].unsqueeze(1)
                        tap = chan[:, kt, C_TAP + HALO - k:C_TAP + HALO - k + 1]
                        if k == 0:
                            op = dve.tensor_scalar(c, x, tap, chan[:, kt, C_CONVB:C_CONVB + 1], ALU.mult, ALU.add)
                        else:
                            dve.wait_ge(s_["taps"], KT * (TAPS * ch + k - 1) + kt + 1)
                            op = dve.scalar_tensor_tensor(out=c, in0=x, scalar=tap, in1=c, op0=ALU.mult, op1=ALU.add)
                        op.then_inc(s_["taps"], 1)
            def skip_product(ch):
                dve.wait_ge(s_["skip_out"], 16 * ch + 16)
                for kt in range(KT):
                    op = dve.tensor_scalar(skip[:, kt, :].unsqueeze(1), xnT[:, ds(ch, 1), kt, HALO:], chan[:, kt, C_D:C_D + 1], None, ALU.mult)
                op.then_inc(s_["skip_done"], 1)

            dve.wait_ge(s_["halo"], 1)
            skip_product(0)
            convolve(0)
            chain = [0]

            def link(op):
                chain[0] += 1
                op.then_inc(s_["route"], 1)
                dve.wait_ge(s_["route"], chain[0])

            def wide(x):
                return x[:].unsqueeze(2).to_broadcast([P, NT, E])

            dve.wait_ge(s_["lg_copied"], NCH + 1)
            link(dve.tensor_reduce(c0[:], logits[:], AX, ALU.max))
            dve.tensor_tensor(rt[0][:], logits[:], wide(c0), ALU.subtract).then_inc(s_["shifted"], 1)
            dve.wait_ge(s_["exped"], 1)
            link(dve.tensor_reduce(c1[:], rt[1][:], AX, ALU.add))
            link(dve.reciprocal(c2[:], c1[:]))
            link(dve.tensor_tensor(rt[2][:], rt[1][:], wide(c2), ALU.mult))
            score = rt[2]
            for s in range(2):
                link(dve.tensor_reduce(best[s][:], score[:], AX, ALU.max))
                link(dve.tensor_tensor(rt[0][:], score[:], wide(best[s]), ALU.is_equal))
                link(dve.tensor_tensor(rt[0][:], rt[0][:], rev[:], ALU.mult))
                link(dve.tensor_reduce(pick[s][:], rt[0][:], AX, ALU.max))
                link(dve.tensor_tensor(mask[s][:], rev[:], wide(pick[s]), ALU.is_equal))
                if s == 0:
                    score = rt[3]
                    link(dve.scalar_tensor_tensor(out=score[:], in0=mask[0][:], scalar=-2.0, in1=rt[2][:], op0=ALU.mult, op1=ALU.add))
            dve.sem_inc(s_["masks"], 1)
            link(dve.tensor_tensor(c0[:], best[0][:], best[1][:], ALU.add))
            link(dve.tensor_scalar(c0[:], c0[:], 1e-9, None, ALU.max))
            link(dve.reciprocal(c1[:], c0[:]))
            for s in range(2):
                link(dve.tensor_tensor(entry[:, s, :, 1], best[s][:], c1[:], ALU.mult))
                link(dve.tensor_copy(entry[:, s, :, 0], tokens[:, 0, :]))
            dve.wait_ge(s_["counted"], 1)
            for s in range(2):
                link(dve.tensor_copy(tot[:], pC[:, s, NT * E:].rearrange("p (t e) -> p e t", e=E)))
                link(dve.tensor_tensor_scan(incl[s][:].rearrange("p e t -> p (e t)"), reset[:].rearrange("p e t -> p (e t)"),
                                            tot[:].rearrange("p e t -> p (e t)"), 0.0, ALU.mult, ALU.add))
                link(dve.tensor_tensor(excl[:], incl[s][:], tot[:], ALU.subtract))
                if s == 1:
                    link(dve.tensor_tensor(excl[:], excl[:], incl[0][:, :, NT - 1:NT].to_broadcast([P, E, NT]), ALU.add))
                link(dve.tensor_tensor(rt[0][:], pC[:, s, 0:NT * E].rearrange("p (t e) -> p t e", e=E), excl[:].rearrange("p e t -> p t e"), ALU.add))
                link(dve.tensor_tensor(rt[0][:], rt[0][:], mask[s][:], ALU.mult))
                link(dve.tensor_reduce(c0[:], rt[0][:], AX, ALU.add))
                link(dve.tensor_scalar(c1[:], pick[s][:], -float(CAP), float(E * CAP - 1), ALU.mult, ALU.add))
                link(dve.tensor_tensor(c1[:], c1[:], c0[:], ALU.add))
                link(dve.tensor_scalar(c2[:], c0[:], float(CAP), None, ALU.is_le))
                link(dve.tensor_tensor(c1[:], c1[:], tokens[:, 1 + s, :], ALU.subtract))
                link(dve.tensor_tensor(c1[:], c1[:], c2[:], ALU.mult))
                link(dve.tensor_tensor(c1[:], c1[:], tokens[:, 1 + s, :], ALU.add))
                link(dve.tensor_copy(place[:, s, :], c1[:]))
            dve.sem_inc(s_["placed"], 1)
            dve.wait_ge(s_["neg_a"], 1)
            link(dve.tensor_scalar(keep["neg_a"][:], keep["neg_a"][:], -1.0, None, ALU.mult))

            def soft(ch):
                for n, h in enumerate(HALVES):
                    dve.wait_ge(s_["expz"], 2 * ch + n + 1)
                    dve.wait_ge(s_["delta"], 2 * ch + 1)
                    dve.tensor_scalar(back[:, h], za[:, h], 1.0, -1.0, ALU.add, ALU.add).then_inc(s_["rounded"], 1)
                h = HALVES[1]
                dve.wait_ge(s_["rounded"], 2 * ch + 2)
                dve.tensor_tensor(back[:, h], za[:, h], back[:, h], ALU.subtract).then_inc(s_["dropped_dve"], 1)
                for h in HALVES[::-1]:
                    dve.wait_ge(s_["dropped" if h.start == 0 else "dropped_dve"], ch + 1)
                    dve.scalar_tensor_tensor(out=back[:, h], in0=z[:, h], scalar=0.0, in1=back[:, h], op0=ALU.max, op1=ALU.add).then_inc(s_["soft"], 1)
                dve.wait_ge(s_["soft"], 2 * ch + 4)
                for n, h in enumerate(HALVES):
                    dve.wait_ge(s_["lnz"], 2 * ch + n + 1)
                    dve.tensor_tensor(ln[:, h], ln[:, h], back[:, h], ALU.add).then_inc(s_["delta"], 1)

            for ch in range(1, AHEAD):
                skip_product(ch)
                convolve(ch)
            with dve.Fori(0, NCH - AHEAD) as ch:
                skip_product(ch + AHEAD)
                convolve(ch + AHEAD)
                soft(ch)
            for ch in range(NCH - AHEAD, NCH - 1):
                soft(ch)
            dve.wait_ge(s_["table"], 16)
            dve.tensor_copy(keep["add_row"][:, 0], vacant[:, 0, :, 0])
            dve.tensor_copy(keep["add_row"][:, 1:], filled[:, :, :, 0])
            dve.tensor_copy(keep["gate"][:], filled[:, :, :, 1])
            dve.tensor_scalar(keep["row"][:, E], vacant[:, 0, :, 0], float(S - 1), None, ALU.min)
            dve.tensor_scalar(keep["row"][:, 0:E], filled[:, :, :, 0], float(S - 1), None, ALU.min).then_inc(s_["indexed"], 1)
            soft(NCH - 1)
            dve.wait_ge(s_["indexed"], 1)


def main_loop(nc, a, dr, keep):
    with ExitStack() as ctx:
        sb, psum, sems = memory(nc, ctx)
        ident = sb("m_ident", [P, P])
        raw = sb("w_raw", [P, KT * QH])
        w1h, w1l = sb("w1h", [P, KT, QH], F32R), sb("w1l", [P, KT, QH], F32R)
        w2h, w2l = sb("w2h", [P, HT, D], F32R), sb("w2l", [P, HT, D], F32R)
        xTh, xTl = sb("xTh", [P, KT, CAP], F32R), sb("xTl", [P, KT, CAP], F32R)
        hh, hl = sb("hh", [P, 2, HT, 512], F32R), sb("hl", [P, 2, HT, 512], F32R)
        part = sb("part", [P, TILES, D])
        b2 = sb("b2_sb", [P, D])
        got = sb("got", [P, 4, D])
        row_now = sb("row_now", [P, TILES], I32)
        add_now = sb("add_now", [P, TILES], I32)
        u, delta, s_acc = sb("u_sb", [P, KT, CH]), sb("delta_sb", [P, KT, CH]), sb("s_acc", [P, KT, CH])
        abuf = sb("a_sb", [P, 8, 2, CH])
        bbuf = sb("b_sb", [P, 2, 2, CH])
        bc = sb("bc_sb", [P, 2, 2, CH])
        state = sb("state", [P, N, KT])
        warm = sb("warm", [P, 2])
        ph = psum("ph", [P, 4, 512])
        pacc = psum("pacc", [P, 3, D])
        ptr = psum("ptr", [P, 512])
        s_ = sems("m_", """ident raw_in w_hi w_lo x_got0 x_got1 x_got2 x_got3 x_turned x_hi x_lo l1 gelu h_free l2
            acc_free exp a_free bmul scan carried product kept bc_in0 bc_in1 d_in u_in0 u_in1 s_out
            b2_in staged add_staged added cleared biased pe_at act_at dve_at pool_at""")
        block = ctx.enter_context(nc.Block())
        NH = 8 * NQ
        LATE = 7

        def chunks(eng, body):
            with eng.Fori(0, B) as b:
                with eng.Fori(0, CPB) as c:
                    body(b * CPB + c)

        def quarters(e, eng, quarter):
            quarter(e * NQ, 0, True, False)
            with eng.Fori(1, NQ - 1) as q:
                quarter(e * NQ + q, q, False, False)
            quarter(e * NQ + NQ - 1, NQ - 1, False, True)

        @block.sync
        def _(sp):
            sp.dma_start(ident[:], a["ident"]).then_inc(s_["ident"], 16)

            def chunk(e):
                def step_bc(q, k):
                    m = e * N + q * 4 + k
                    sp.wait_ge(s_["product"], 2 * m + 2)
                    n = q * 4 + k
                    src = dr.bc[ds(e, 1)].rearrange("o (w n) t -> n (o w) t", w=2)[ds(n, 1)]
                    sp.dma_start(bc[:, k % 2], src.to_broadcast([P, 2, CH])).then_inc(s_[f"bc_in{k % 2}"], 16)

                def weights(it, which):
                    sp.wait_ge(s_["w_lo"], 2 * it + which + 1)
                    sp.wait_ge(s_["w_hi"], 2 * it + which + 1)
                    src = a["w1" if which == 0 else "w2"][ds(it, 1)].rearrange("o p f -> p (o f)")
                    sp.dma_start(raw[:], src).then_inc(s_["raw_in"], 16)

                def load_u(h):
                    sp.wait_ge(s_["bmul"], NH * e + 1 + h)
                    sp.dma_start(u[:, 2 * h:2 * h + 2], dr.u[ds(e, 1), :, 2 * h:2 * h + 2, :].rearrange("o p k t -> p (o k) t")).then_inc(s_[f"u_in{h}"], 16)

                def quarter(it, q, first, last):
                    weights(it, 0)
                    if first:
                        sp.wait_ge(s_["exp"], NH * e + 1)
                        sp.dma_start(delta[:], dr.delta[ds(e, 1)].rearrange("o p k t -> p (o k) t")).then_inc(s_["d_in"], 16)
                        load_u(0)
                    step_bc(q, 0)
                    if first:
                        load_u(1)
                        sp.wait_ge(s_["biased"], TILES * e + 1)
                        sp.dma_start(b2[:], a["fc2_b"][ds(e, 1)].to_broadcast([P, D])).then_inc(s_["b2_in"], 16)
                    weights(it, 1)
                    for k in range(1, 4):
                        step_bc(q, k)

                quarters(e, sp, quarter)

            chunks(sp, chunk)

        @block.tensor
        def _(pe):
            for name, credits in (("x_turned", 4), ("l1", 1), ("l2", 1)):
                pe.sem_inc(s_[name], credits)
            pe.wait_ge(s_["ident"], 16)

            def three(out, stat, mov, start, stop):
                (sh, sl), (mh, ml) = stat, mov
                pe.matmul(out, sl, mh, start=start, stop=False)
                pe.matmul(out, sh, ml, start=False, stop=False)
                return pe.matmul(out, sh, mh, start=False, stop=stop)

            def turn(e, t):
                pe.wait_ge(s_[f"x_got{t % 4}"], 16 * (2 * e + t // 4) + 16)
                pe.wait_ge(s_["x_lo"], TILES * e + t + 2)
                for kt in range(KT):
                    mm = pe.transpose(ptr[:, kt * P:(kt + 1) * P], got[:, t % 4, kt * P:(kt + 1) * P], ident[:])
                mm.then_inc(s_["x_turned"], 1)

            for t in range(TILES):
                turn(0, t)

            def chunk(e):
                def quarter(it, q, first, last):
                    pe.wait_ge(s_["w_lo"], 2 * it + 2)
                    for g in range(2):
                        if first:
                            pe.wait_ge(s_["x_lo"], TILES * e + 4 * g + 6)
                        for j in range(HT):
                            pe.wait_ge(s_["h_free"], 8 * it + 4 * g + j + 1)
                            for kt in range(KT):
                                w = (w1h[:, kt, j * P:(j + 1) * P], w1l[:, kt, j * P:(j + 1) * P])
                                x = (xTh[:, kt, g * 512:(g + 1) * 512], xTl[:, kt, g * 512:(g + 1) * 512])
                                mm = three(ph[:, j, :], w, x, kt == 0, kt == KT - 1)
                            mm.then_inc(s_["l1"], 1)
                    pe.wait_ge(s_["w_lo"], 2 * it + 3)
                    for t in range(TILES):
                        g, c = t // 4, (t % 4) * P
                        pe.wait_ge(s_["h_free"], 8 * it + 4 * g + 8)
                        if t != 2:
                            pe.wait_ge(s_["acc_free"], 8 * it + (t if t > 2 else t + 1))
                        for j in range(HT):
                            mm = three(pacc[:, t % 3, :], (hh[:, g, j, c:c + P], hl[:, g, j, c:c + P]),
                                       (w2h[:, j, :], w2l[:, j, :]), j == 0, j == HT - 1)
                        mm.then_inc(s_["l2"], 1)
                        if last:
                            turn(e + 1, t)

                quarters(e, pe, quarter)

            chunks(pe, chunk)

        @block.scalar
        def _(act):
            act.sem_inc(s_["w_hi"], 1)
            act.sem_inc(s_["exp"], 1)
            act.wait_ge(s_["cleared"], 3)

            def split_x(e, t):
                act.wait_ge(s_["x_turned"], TILES * e + t + 5)
                act.activation(xTh[:, :, t * P:(t + 1) * P], ptr[:].rearrange("p (k s) -> p k s", k=KT), ACT.Copy).then_inc(s_["x_hi"], 1)

            def chunk(e):
                def split_w(it, which):
                    hi = w1h if which == 0 else w2h
                    act.wait_ge(s_["raw_in"], 16 * (2 * it + which) + 16)
                    act.wait_ge(s_["l1" if which == 0 else "l2"], 8 * it + 1)
                    act.activation(hi[:].rearrange("p k f -> p (k f)"), raw[:], ACT.Copy).then_inc(s_["w_hi"], 1)

                def quarter(it, q, first, last):
                    def exp(i):
                        act.wait_ge(s_["a_free"], 8 * it + i + 1)
                        for k in range(2):
                            kt = 2 * (i % 2) + k
                            col = q * 16 + (i // 2) * 4 + kt
                            op = act.activation(abuf[:, i, k, :], delta[:, kt, :], ACT.Exp,
                                                scale=keep["neg_a"][:].rearrange("p n k -> p (n k)")[:, ds(col, 1)])
                        op.then_inc(s_["exp"], 1)

                    lag = 2 if first else 0
                    for i in range(LATE + lag):
                        if first and i < TILES:
                            split_x(e, i)
                        if first and i == lag:
                            act.wait_ge(s_["d_in"], 16 * e + 16)
                        if i >= lag:
                            exp(i - lag)
                        if i == 3:
                            split_w(it, 0)
                    act.activation(warm[:, 1:2], warm[:, 0:1], ACT.Gelu)
                    for g in range(2):
                        for j in range(HT):
                            act.wait_ge(s_["l1"], 8 * it + 4 * g + j + 2)
                            apart(act, s_["act_at"])
                            bias = keep["b1"][:, ds(4 * it + j, 1)]
                            act.activation(hh[:, g, j, :], ph[:, j, :], ACT.Gelu, bias=bias)
                            act.activation(ph[:, j, :], ph[:, j, :], ACT.Gelu, bias=bias).then_inc(s_["gelu"], 1)
                            if g == 0 and j == 1:
                                split_w(it, 1)
                        if g == 0:
                            for i in range(LATE, 8):
                                exp(i)

                quarters(e, act, quarter)

            chunks(act, chunk)
            for t in range(TILES):
                split_x(NCH, t)

        @block.gpsimd
        def _(pool):
            pool.sem_inc(s_["w_lo"], 1)
            pool.sem_inc(s_["bmul"], 2)

            def stage_rows(e):
                pool.wait_ge(s_["x_turned"], TILES * e + 4)
                pool.tensor_copy(row_now[:], keep["row"][:, ds(e, 1), :].rearrange("p o j -> p (o j)")).then_inc(s_["staged"], 1)

            def gather(e, t):
                pool.wait_ge(s_["staged"], e + 1)
                pool.wait_ge(s_["x_turned"], TILES * e + t + 1)
                apart(pool, s_["pool_at"])
                pool.indirect_dma_start(got[:, t % 4, :], None, dr.xn, bass.IndirectOffsetOnAxis(ap=row_now[:, t:t + 1], axis=0)).then_inc(s_[f"x_got{t % 4}"], 16)

            def add_sum(e):
                pool.wait_ge(s_["a_free"], NH * e + 8)
                apart(pool, s_["pool_at"])
                pool.dma_start(dr.s[ds(e, 1)].rearrange("o p k t -> p (o k) t"), s_acc[:], accum_op=ALU.add).then_inc(s_["s_out"], 16)

            def stage_adds(e):
                pool.wait_ge(s_["acc_free"], 8 * NQ * e + 2)
                pool.tensor_copy(add_now[:], keep["add_row"][:, ds(e, 1), :].rearrange("p o j -> p (o j)")).then_inc(s_["add_staged"], 1)
                pool.wait_ge(s_["add_staged"], e + 1)
                apart(pool, s_["pool_at"])

            def add_tile(t):
                pool.indirect_dma_start(dr.y, bass.IndirectOffsetOnAxis(ap=add_now[:, t:t + 1], axis=0), part[:, t, :], None,
                                        compute_op=ALU.add).then_inc(s_["added"], 16)

            ADDS = {1: (0, 1), 2: (2, 3), 3: (4, 5, 6), 4: (7,)}
            GATHERS = {1: (0, 1), 2: (2,), 3: (3,), 5: (4, 5), 6: (6,), 7: (7,)}

            stage_rows(0)
            for t in range(TILES):
                gather(0, t)

            def chunk(e):
                def quarter(it, q, first, last):
                    def low(which):
                        hi, lo = ((w1h, w1l), (w2h, w2l))[which]
                        pool.wait_ge(s_["w_hi"], 2 * it + which + 2)
                        pool.tensor_tensor(lo[:].rearrange("p k f -> p (k f)"), raw[:], hi[:].rearrange("p k f -> p (k f)").bitcast(F32), ALU.subtract).then_inc(s_["w_lo"], 1)

                    low(0)
                    for i in range(8):
                        m = i // 2
                        if first and i < 2:
                            pool.wait_ge(s_[f"u_in{i}"], 16 * e + 16)
                        if i % 2 == 0:
                            pool.wait_ge(s_[f"bc_in{m % 2}"], 16 * (2 * it + m // 2) + 16)
                        pool.wait_ge(s_["scan"], 8 * it + i + 1)
                        h = 2 * (i % 2)
                        pool.tensor_tensor(bbuf[:, i % 2], u[:, h:h + 2, :], bc[:, m % 2, 0:1, :].to_broadcast([P, 2, CH]), ALU.mult).then_inc(s_["bmul"], 1)
                        if i == 2:
                            low(1)
                        if first:
                            if i == 1:
                                add_sum(e)
                                stage_adds(e)
                            for t in ADDS.get(i, ()):
                                add_tile(t)
                        if last:
                            if i == 0:
                                stage_rows(e + 1)
                            for t in GATHERS.get(i, ()):
                                gather(e + 1, t)

                quarters(e, pool, quarter)

            chunks(pool, chunk)
            pool.tensor_copy(add_now[:], keep["add_row"][:, NCH, :]).then_inc(s_["add_staged"], 1)
            pool.wait_ge(s_["add_staged"], NCH + 1)
            for t in range(TILES):
                pool.wait_ge(s_["acc_free"], 8 * NQ * NCH - 8 + t + 3)
                add_tile(t)
            add_sum(NCH)
            pool.wait_ge(s_["s_out"], 16 * (NCH + 1))
            pool.wait_ge(s_["added"], 16 * TILES * (NCH + 1))

        @block.vector
        def _(dve):
            dve.memset(part[:], 0.0).then_inc(s_["cleared"], 1)
            dve.memset(s_acc[:], 0.0).then_inc(s_["cleared"], 1)
            dve.memset(warm[:], 0.0).then_inc(s_["cleared"], 1)
            dve.wait_ge(s_["cleared"], 3)
            for name, credits in (("x_lo", 2), ("h_free", 4), ("acc_free", 2), ("a_free", 8), ("scan", 2),
                                  ("product", 4), ("biased", 1)):
                dve.sem_inc(s_[name], credits)

            def low_x(e, t):
                dve.wait_ge(s_["x_hi"], TILES * e + t + 1)
                dve.tensor_tensor(xTl[:, :, t * P:(t + 1) * P], ptr[:].rearrange("p (k s) -> p k s", k=KT),
                                  xTh[:, :, t * P:(t + 1) * P].bitcast(F32), ALU.subtract).then_inc(s_["x_lo"], 1)

            for t in range(TILES):
                low_x(0, t)

            def chunk(e):
                def low_h(it, s):
                    g, j = s // 4, s % 4
                    dve.wait_ge(s_["gelu"], 8 * it + s + 1)
                    dve.tensor_tensor(hl[:, g, j, :], ph[:, j, :], hh[:, g, j, :].bitcast(F32), ALU.subtract).then_inc(s_["h_free"], 1)

                def add_part(it, t, first):
                    gate = keep["gate"][:].rearrange("p e j -> p (e j)")[:, ds(8 * e + t, 1)]
                    if first:
                        if t == 0:
                            dve.wait_ge(s_["added"], 16 * TILES * e + 16 * TILES)
                            dve.wait_ge(s_["b2_in"], 16 * e + 16)
                        dve.tensor_scalar(part[:, t, :], b2[:], gate, None, ALU.mult).then_inc(s_["biased"], 1)
                        dve.wait_ge(s_["biased"], TILES * e + t + 2)
                    dve.wait_ge(s_["l2"], 8 * it + t + 2)
                    dve.scalar_tensor_tensor(out=part[:, t, :], in0=pacc[:, t % 3, :], scalar=gate, in1=part[:, t, :],
                                             op0=ALU.mult, op1=ALU.add).then_inc(s_["acc_free"], 1)

                def sum_up(it, i, first):
                    if first and i < 2:
                        return
                    dve.wait_ge(s_["product"], 8 * it + i + 5)
                    acc = s_acc[:, 2 * (i % 2):2 * (i % 2) + 2, :]
                    if first and i < 4:
                        if i == 2:
                            dve.wait_ge(s_["s_out"], 16 * e + 16)
                        dve.tensor_tensor(acc, abuf[:, i - 2], abuf[:, i], ALU.add).then_inc(s_["a_free"], 1 if i == 2 else 3)
                    else:
                        dve.tensor_tensor(acc, acc, abuf[:, i], ALU.add).then_inc(s_["a_free"], 1)

                def quarter(it, q, first, last):
                    st = state[:].rearrange("p n k -> p (n k)")
                    for s in range(16):
                        i, hs = s // 2, 8 * it + s // 2
                        m, kt0 = i // 2, 2 * (i % 2)
                        if s % 2 == 0:
                            dve.wait_ge(s_["exp"], hs + 2)
                            dve.wait_ge(s_["bmul"], hs + 3)
                            for k in range(2):
                                col = q * 16 + m * 4 + kt0 + k
                                op = dve.tensor_tensor_scan(abuf[:, i, k, :], abuf[:, i, k, :], bbuf[:, i % 2, k, :],
                                                            st[:, ds(col, 1)], ALU.mult, ALU.add)
                            op.then_inc(s_["scan"], 1)
                            if i > 0:
                                sum_up(it, i - 1, first)
                            elif not first:
                                sum_up(it - 1, 7, False)
                        else:
                            dve.wait_ge(s_["scan"], hs + 3)
                            apart(dve, s_["dve_at"])
                            dve.tensor_copy(st[:, ds(q * 16 + m * 4 + kt0, 2)].unsqueeze(2), abuf[:, i, :, CH - 1:CH]).then_inc(s_["carried"], 1)
                        if s < 8:
                            low_h(it, s)
                        else:
                            if last:
                                low_x(e + 1, s - 8)
                            add_part(it, s - 8, first)
                        if s % 2 == 1:
                            dve.wait_ge(s_["carried"], hs + 1)
                            dve.tensor_tensor(abuf[:, i], abuf[:, i], bc[:, m % 2, 1:2, :].to_broadcast([P, 2, CH]), ALU.mult).then_inc(s_["product"], 1)
                    if last:
                        sum_up(it, 7, False)

                quarters(e, dve, quarter)

            with dve.Fori(0, B) as b:
                dve.memset(state[:], 0.0).then_inc(s_["kept"], 1)
                dve.wait_ge(s_["kept"], b + 1)
                apart(dve, s_["dve_at"])
                with dve.Fori(0, CPB) as c:
                    chunk(b * CPB + c)


def tail(nc, a, dr, out):
    with ExitStack() as ctx:
        sb, psum, sems = memory(nc, ctx)
        ident = sb("t_ident", [P, P])
        sT = sb("t_sT", [P, 2, KT, CH])
        y, x = sb("t_y", [P, 2, TPC, D]), sb("t_x", [P, 2, TPC, D])
        g, o = sb("t_g", [P, 2, TPC, D]), sb("t_o", [P, 2, TPC, D])
        ps = psum("t_s", [P, 2, TPC, D])
        s_ = sems("t_", "ident in0 in1 turned silu prod sum out0 out1")
        block = ctx.enter_context(nc.Block())

        def over_pairs(eng, body):
            with eng.Fori(0, NCH // 2) as i:
                for u in range(2):
                    body(2 * i + u, i, u)

        @block.sync
        def _(sp):
            sp.dma_start(ident[:], a["ident"]).then_inc(s_["ident"], 16)

            for u in range(2):
                sp.sem_inc(s_[f"out{u}"], 16)

            def load(ch, u):
                sp.wait_ge(s_["sum"], ch + 1)
                sp.dma_start(sT[:, u], dr.s[ds(ch + 1, 1)].rearrange("o p k t -> p (o k) t")).then_inc(s_[f"in{u}"], 16)
                sp.dma_start(y[:, u], dr.y[ds(ch * CH, CH)].rearrange("(j p) d -> p j d", p=P)).then_inc(s_[f"in{u}"], 16)
                sp.dma_start(x[:, u], a["x"][ds(ch, 1)].rearrange("o p j d -> p (o j) d")).then_inc(s_[f"in{u}"], 16)

            def store(ch, u):
                sp.wait_ge(s_["sum"], ch + 3)
                sp.dma_start(out[ds(ch, 1)].rearrange("o (j p) d -> p (o j) d", p=P), o[:, u]).then_inc(s_[f"out{u}"], 16)

            for u in range(2):
                load(u, u)
            with sp.Fori(1, NCH // 2) as i:
                for u in range(2):
                    store(2 * i + u - 2, u)
                    load(2 * i + u, u)
            for u in range(2):
                store(NCH - 2 + u, u)
            for u in range(2):
                sp.wait_ge(s_[f"out{u}"], 16 * NCH // 2 + 16)

        @block.tensor
        def _(pe):
            pe.wait_ge(s_["ident"], 16)

            def turn(ch, i, u):
                pe.wait_ge(s_[f"in{u}"], 48 * i + 48)
                pe.wait_ge(s_["prod"], ch + 1)
                for j in range(TPC):
                    for kt in range(KT):
                        mm = pe.transpose(ps[:, u, j, kt * P:(kt + 1) * P], sT[:, u, kt, j * P:(j + 1) * P], ident[:])
                mm.then_inc(s_["turned"], 1)

            over_pairs(pe, turn)

        @block.scalar
        def _(act):
            def silu(ch, i, u):
                act.wait_ge(s_[f"in{u}"], 48 * i + 48)
                act.wait_ge(s_["prod"], ch + 1)
                act.activation(g[:, u], y[:, u], ACT.Silu).then_inc(s_["silu"], 1)

            over_pairs(act, silu)

        @block.vector
        def _(dve):
            dve.sem_inc(s_["sum"], 2)
            dve.sem_inc(s_["prod"], 2)

            def combine(ch, i, u):
                dve.wait_ge(s_["silu"], ch + 1)
                dve.wait_ge(s_["turned"], ch + 1)
                dve.wait_ge(s_[f"out{u}"], 16 * i + 16)
                dve.tensor_tensor(o[:, u], ps[:, u], g[:, u], ALU.mult).then_inc(s_["prod"], 1)
                dve.wait_ge(s_["prod"], ch + 3)
                dve.tensor_tensor(o[:, u], o[:, u], x[:, u], ALU.add).then_inc(s_["sum"], 1)

            over_pairs(dve, combine)


def build(nc, a, out):
    dr = Scratch(nc)
    with ExitStack() as ctx:
        sb, _, _ = memory(nc, ctx)
        keep = {
            "b1": sb("b1_keep", [P, E * HID // P]),
            "neg_a": sb("neg_a_keep", [P, N, KT]),
            "row": sb("row_keep", [P, E + 1, TILES], I32),
            "add_row": sb("add_row_keep", [P, E + 1, TILES], I32),
            "gate": sb("gate_keep", [P, E, TILES]),
        }
        front(nc, a, dr, keep)
        main_loop(nc, a, dr, keep)
    tail(nc, a, dr, out)


def lay_out(i):
    def per_channel(x):
        return x.reshape(KT, P, -1).transpose(1, 0, 2)

    chan = np.concatenate([per_channel(x) for x in (
        i["L0_attn_conv_w"].reshape(D, TAPS), i["L0_attn_conv_b"], i["L0_attn_dtproj_b"], i["L0_attn_D_param"], i["L0_attn_A_log"])], axis=2)
    w1 = i["L0_ffn_fc1_w"].reshape(E, KT, P, NQ, QH).transpose(0, 3, 2, 1, 4)
    w2 = i["L0_ffn_fc2_w"].reshape(E, NQ, HT, P, D).transpose(0, 1, 3, 2, 4)
    return {
        "x": i["L0_attn_x"].reshape(NCH, TPC, P, D).transpose(0, 2, 1, 3),
        "chan": chan,
        "xprojT": i["L0_attn_xproj_w"].T.reshape(KT, P, R + 2 * N).transpose(1, 0, 2),
        "dtprojT": i["L0_attn_dtproj_w"].T,
        "wg": i["L0_ffn_wg"].reshape(KT, P, E).transpose(1, 0, 2),
        "w1": w1.reshape(E * NQ, P, KT * QH),
        "w2": w2.reshape(E * NQ, P, HT * D),
        "fc1_b": i["L0_ffn_fc1_b"].reshape(E * HID // P, P).T,
        "fc2_b": i["L0_ffn_fc2_b"],
    }


def constants():
    f = np.float32
    token = (np.arange(NT)[None, :] * P + np.arange(P)[:, None]).astype(f)
    slot = np.arange(CAP).reshape(P, TILES)
    vacant = np.zeros((P, E, TILES, 2), f)
    vacant[..., 0] = (S + slot)[:, None, :]
    reset = np.ones((P, E, NT), f)
    reset[:, :, 0] = 0
    return {
        "ident": np.eye(P, dtype=f),
        "tri": np.triu(np.ones((P, P), f)),
        "ones": np.ones((P, P), f),
        "rev": np.broadcast_to((E - np.arange(E)).astype(f), (P, NT, E)),
        "reset": reset,
        "tokens": np.stack([token, TRASH + token, TRASH + S + token], axis=1),
        "mhalf": np.full((P, TPC), -0.5, f),
        "vacant": vacant,
    }


def kernel(**inputs):
    import concourse.bacc as bacc
    from concourse.bass_utils import run_bass_kernel_spmd

    nc = bacc.Bacc("TRN2", target_bir_lowering=False, num_devices=1)
    given = lay_out({k: np.asarray(v) for k, v in inputs.items()})
    given.update(constants())
    arrays, aps = {}, {}
    for name, value in given.items():
        value = np.ascontiguousarray(value)
        arrays[f"in_{name}"] = value
        aps[name] = nc.dram_tensor(f"in_{name}", value.shape, mybir.dt.from_np(value.dtype), kind="ExternalInput").ap()
    out = nc.dram_tensor("out", (NCH, CH, D), F32, kind="ExternalOutput").ap()
    build(nc, aps, out)
    r = run_bass_kernel_spmd(nc, [arrays], core_ids=[0])
    return np.asarray(r.results[0]["out"]).reshape(B, T, D)
```

```python
from contextlib import ExitStack

import numpy as np

import concourse.bass as bass
from concourse import mybir

F32 = mybir.dt.float32
F32R = mybir.dt.float32r
I32 = mybir.dt.int32
ALU = mybir.AluOpType
ACT = mybir.ActivationFunctionType
AX = mybir.AxisListType.X
ds = bass.ds

P = 128
B, T, D = 2, 2048, 512
S = B * T
KT = D // P
N = 16
TAPS = 4
R = 128
E, HID = 8, 2048
CAP = 2 * S // E
CH = 512
NCH = S // CH
CPB = T // CH
TPC = CH // P
NT = S // P
TILES = CAP // P
QH = 512
NQ = HID // QH
HT = QH // P
HALO = TAPS - 1
EPS = 1e-5
TRASH = E * CAP
C_TAP, C_CONVB, C_DTB, C_ALOG = 0, TAPS, TAPS + 1, TAPS + 2


class Scratch:

    def __init__(self, nc):
        def dram(name, shape):
            return nc.dram_tensor(name, shape, F32).ap()

        self.xn = dram("xn_rows", (S, D))
        self.slots = dram("slot_table", (E * CAP + 2 * S, 2))
        self.y = dram("moe_rows", (S + CAP, D))
        self.delta = dram("delta_chunks", (NCH, P, KT, CH))
        self.u = dram("u_chunks", (NCH, P, KT, CH))
        self.bc = dram("bc_chunks", (NCH, 2 * N, CH))
        self.s = dram("s_chunks", (NCH + 1, P, KT, CH))


def memory(nc, ctx):
    def sb(name, shape, dt=F32):
        return ctx.enter_context(nc.sbuf_tensor(name, shape, dt))

    def psum(name, shape):
        return ctx.enter_context(nc.psum_tensor(name, shape, F32))

    def sems(prefix, names):
        return {n: ctx.enter_context(nc.semaphore(prefix + n)) for n in names.split()}

    return sb, psum, sems


def apart(eng, sem):
    eng.sem_inc(sem, 1)


def front(nc, a, dr, keep):
    with ExitStack() as ctx:
        sb, psum, sems = memory(nc, ctx)
        ident, tri, ones = sb("f_ident", [P, P]), sb("f_tri", [P, P]), sb("f_ones", [P, P])
        wg = sb("wg_sb", [P, KT, E])
        xprojT = sb("xprojT_sb", [P, KT, R + 2 * N])
        dtprojT = sb("dtprojT_sb", [P, D])
        chan = sb("chan_sb", [P, KT, C_ALOG + N])
        rev, reset = sb("rev_sb", [P, NT, E]), sb("reset_sb", [P, E, NT])
        tokens = sb("tokens_sb", [P, 3, NT])
        mhalf = sb("mhalf_sb", [P, TPC])
        vacant = sb("vacant_sb", [P, E, TILES, 2])
        filled = sb("filled_sb", [P, E, TILES, 2])
        xin = sb("xin_sb", [P, 2, TPC, D])
        xn = sb("xn_sb", [P, 2, TPC, D])
        stats = sb("stats_sb", [P, TPC, 6])
        moments = sb("moments_sb", [P, 2, TPC, 2])
        xnT = sb("xnT_sb", [P, NCH + 1, KT, HALO + CH])
        lgT = sb("lgT_sb", [E, CH])
        logits = sb("logits_sb", [P, NT, E])
        zeros, warm = sb("zeros_sb", [P, 512]), sb("f_warm", [P, 1])
        conv = sb("conv_sb", [P, KT, CH])
        dtin = sb("dtin_sb", [P, CH])
        bcrows = sb("bcrows_sb", [2 * N, CH])
        za, z = sb("za_sb", [P, KT, CH]), sb("z_sb", [P, KT, CH])
        ln = sb("ln_sb", [P, KT, CH])
        back = sb("back_sb", [P, KT, CH])
        u_now = sb("u_now_sb", [P, KT, CH])
        rt = [sb(f"rt{i}", [P, NT, E]) for i in range(4)]
        mask = [sb(f"mask{s}", [P, NT, E]) for s in range(2)]
        excl = sb("excl_sb", [P, E, NT])
        incl = [sb(f"incl{s}", [P, E, NT]) for s in range(2)]
        tot = sb("tot_sb", [P, E, NT])
        best = [sb(f"best{s}", [P, NT]) for s in range(2)]
        pick = [sb(f"pick{s}", [P, NT]) for s in range(2)]
        c0, c1, c2 = (sb(f"c{i}", [P, NT]) for i in range(3))
        entry = sb("entry_sb", [P, 2, NT, 2])
        place = sb("place_sb", [P, 2, NT], I32)

        pT = psum("pT", [P, 4, CH])
        pX = psum("pX", [P, 2, CH])
        pC = psum("pC", [P, 2, CH])

        s_ = sems("f_", """early consts x_in0 x_in1 xn_out0 xn_out1 cleared stats moments power normed xT xT_copied
            lgT lgT_copied lg lg_copied route shifted exped masks counted placed defaults scattered table
            indexed zeroed halo taps silu proj dtin bc_rows bc_out dt dt_read absz expz
            lnz rounded dropped dropped_dve soft delta u_done delta_out u_out neg_a
            pe_at act_at dve_at sp_at pool_at""")

        early = ((ident, "ident"), (wg, "wg"), (mhalf, "mhalf"))
        consts = ((tri, "tri"), (ones, "ones"), (chan, "chan"), (rev, "rev"),
                  (reset, "reset"), (tokens, "tokens"), (xprojT, "xprojT"), (dtprojT, "dtprojT"),
                  (vacant, "vacant"), (keep["b1"], "fc1_b"))
        HALVES = (slice(0, KT // 2), slice(KT // 2, KT))
        FIRST_SCATTERS, NEXT_SCATTERS = 24, 7
        AHEAD = 2
        block = ctx.enter_context(nc.Block())

        def over_pairs(eng, body):
            with eng.Fori(0, NCH // 2) as i:
                for u in range(2):
                    body(2 * i + u, i, u)

        @block.sync
        def _(sp):
            for name, credits in (("xn_out0", 16), ("xn_out1", 16), ("delta_out", 16), ("u_out", 32)):
                sp.sem_inc(s_[name], credits)

            def load(ch, u):
                sp.wait_ge(s_["normed"], ch + 1)
                sp.dma_start(xin[:, u], a["x"][ds(ch, 1)].rearrange("o p j d -> p (o j) d")).then_inc(s_[f"x_in{u}"], 16)

            def store(ch, u):
                sp.wait_ge(s_["normed"], ch + 3)
                sp.dma_start(dr.xn[ds(ch * CH, CH)].rearrange("(j p) d -> p j d", p=P), xn[:, u]).then_inc(s_[f"xn_out{u}"], 16)

            for u in range(2):
                load(u, u)
            for name, group in (("early", early), ("consts", consts)):
                for dst, src in group:
                    sp.dma_start(dst[:], a[src]).then_inc(s_[name], 16)
            with sp.Fori(1, NCH // 2) as i:
                for u in range(2):
                    load(2 * i + u, u)
                    store(2 * i + u - 2, u)
            for u in range(2):
                store(NCH - 2 + u, u)
            sp.wait_ge(s_["cleared"], 1)
            sp.wait_ge(s_["consts"], 16 * len(consts))
            sp.dma_start(dr.slots[0:TRASH].rearrange("(e p j) k -> p e j k", p=P, j=TILES), vacant[:]).then_inc(s_["defaults"], 16)
            for r in range(0, (S + CAP) // P, 8):
                sp.dma_start(dr.y[r * P:(r + 8) * P].rearrange("(r p) d -> p r d", p=P),
                             zeros[:].unsqueeze(1).to_broadcast([P, 8, D])).then_inc(s_["zeroed"], 16)

            def store_du(ch):
                sp.wait_ge(s_["delta"], 2 * ch + 3)
                apart(sp, s_["sp_at"])
                sp.dma_start(dr.delta[ds(ch, 1)].rearrange("o p k t -> p (o k) t"), ln[:]).then_inc(s_["delta_out"], 16)
                for n, h in enumerate(HALVES):
                    sp.wait_ge(s_["u_done"], 2 * ch + n + 2)
                    apart(sp, s_["sp_at"])
                    sp.dma_start(dr.u[ds(ch, 1), :, h].rearrange("o p k t -> p (o k) t"), u_now[:, h]).then_inc(s_["u_out"], 16)

            with sp.Fori(0, NCH - AHEAD) as ch:
                store_du(ch)
            sp.wait_ge(s_["scattered"], 16 * 2 * NT)
            sp.dma_start(filled[:], dr.slots[0:TRASH].rearrange("(e p j) k -> p e j k", p=P, j=TILES)).then_inc(s_["table"], 16)
            for ch in range(NCH - AHEAD, NCH):
                store_du(ch)
            sp.wait_ge(s_["zeroed"], 16 * ((S + CAP) // P // 8))
            sp.wait_ge(s_["xn_out0"], 16 * NCH // 2 + 16)
            sp.wait_ge(s_["xn_out1"], 16 * NCH // 2 + 16)
            sp.wait_ge(s_["delta_out"], 16 * NCH + 16)
            sp.wait_ge(s_["u_out"], 32 * NCH + 32)

        @block.tensor
        def _(pe):
            for name, credits in (("xT", KT + 1), ("lg", 1), ("proj", 1), ("dt", 1)):
                pe.sem_inc(s_[name], credits)
            pe.wait_ge(s_["early"], 16 * len(early))

            def turn(ch, u, i):
                pe.wait_ge(s_["normed"], ch + 3)
                for kt in range(KT):
                    pe.wait_ge(s_["xT_copied"], KT * ch + kt + 1)
                    for j in range(TPC):
                        mm = pe.transpose(pT[:, kt, j * P:(j + 1) * P], xn[:, u, j, kt * P:(kt + 1) * P], ident[:])
                    mm.then_inc(s_["xT"], 1)

            def logits_T(ch):
                pe.wait_ge(s_["xT_copied"], KT * ch + 2 * KT)
                pe.wait_ge(s_["lgT_copied"], ch + 1)
                for kt in range(KT):
                    mm = pe.matmul(pX[0:E, 0, :], wg[:, kt, :], xnT[:, ds(ch, 1), kt, HALO:], start=(kt == 0), stop=(kt == KT - 1))
                mm.then_inc(s_["lgT"], 1)

            def turn_logits(ch):
                pe.wait_ge(s_["lgT_copied"], ch + 2)
                pe.wait_ge(s_["lg_copied"], ch + 1)
                apart(pe, s_["pe_at"])
                for j in range(TPC):
                    mm = pe.transpose(pX[:, 1, j * E:(j + 1) * E], lgT[:, j * P:(j + 1) * P], ident[0:E, 0:E])
                mm.then_inc(s_["lg"], 1)

            turn(0, 0, 0)
            with pe.Fori(0, NCH // 2 - 1) as i:
                for u in range(2):
                    logits_T(2 * i + u)
                    turn(2 * i + u + 1, 1 - u, i)
                    turn_logits(2 * i + u)
            logits_T(NCH - 2)
            turn(NCH - 1, 1, 0)
            turn_logits(NCH - 2)
            logits_T(NCH - 1)
            turn_logits(NCH - 1)

            pe.wait_ge(s_["consts"], 16 * len(consts))
            pe.wait_ge(s_["masks"], 1)
            pe.wait_ge(s_["lg_copied"], NCH + 1)
            for s in range(2):
                for k, w in enumerate((tri, ones)):
                    mm = pe.matmul(pC[:, s, k * NT * E:(k + 1) * NT * E], w[:], mask[s][:].rearrange("p t e -> p (t e)"), start=True, stop=True)
            mm.then_inc(s_["counted"], 1)

            def project(ch):
                pe.wait_ge(s_["bc_rows"], ch + 1)
                for kt in range(KT):
                    pe.wait_ge(s_["silu"], KT * ch + kt + 2)
                    xs = xnT[:, ds(ch, 1), kt, HALO:]
                    pe.matmul(pX[:, 0, :], xprojT[:, kt, 0:R], xs, start=(kt == 0), stop=(kt == KT - 1))
                    mm = pe.matmul(pX[0:2 * N, 1, :], xprojT[:, kt, R:R + 2 * N], xs, start=(kt == 0), stop=(kt == KT - 1))
                mm.then_inc(s_["proj"], 1)

            def widen_dt(ch):
                pe.wait_ge(s_["dtin"], ch + 1)
                for kt in range(KT):
                    pe.wait_ge(s_["dt_read"], KT * ch + kt + 1)
                    pe.matmul(pT[:, kt, :], dtprojT[:, kt * P:(kt + 1) * P], dtin[:], start=True, stop=True).then_inc(s_["dt"], 1)

            with pe.Fori(0, NCH) as ch:
                project(ch)
                widen_dt(ch)

        @block.scalar
        def _(act):
            for name, credits in (("xT_copied", KT), ("lgT_copied", 1), ("lg_copied", 1), ("silu", 1), ("bc_rows", 1),
                                  ("dt_read", KT), ("bc_out", 16)):
                act.sem_inc(s_[name], credits)

            def copy_xT(ch):
                for kt in range(KT):
                    act.wait_ge(s_["xT"], KT * ch + KT + kt + 2)
                    act.activation(xnT[:, ds(ch, 1), kt, HALO:], pT[:, kt, :].unsqueeze(1), ACT.Copy)
                    act.activation(xnT[:, ds(ch + 1, 1), kt, 0:HALO], pT[:, kt, CH - HALO:].unsqueeze(1), ACT.Copy).then_inc(s_["xT_copied"], 1)

            def copy_lgT(ch):
                act.wait_ge(s_["lgT"], ch + 1)
                act.wait_ge(s_["lg"], ch + 1)
                act.activation(lgT[:], pX[0:E, 0, :], ACT.Copy).then_inc(s_["lgT_copied"], 1)

            def copy_lg(ch):
                act.wait_ge(s_["lg"], ch + 2)
                act.activation(logits[:, ds(TPC * ch, TPC), :], pX[:, 1, 0:TPC * E].rearrange("p (j e) -> p j e", e=E), ACT.Copy).then_inc(s_["lg_copied"], 1)

            copy_xT(0)
            with act.Fori(0, NCH - 1) as ch:
                copy_lgT(ch)
                copy_xT(ch + 1)
                copy_lg(ch)
            copy_lgT(NCH - 1)
            copy_lg(NCH - 1)

            act.wait_ge(s_["consts"], 16 * len(consts))
            act.wait_ge(s_["cleared"], 1)
            act.wait_ge(s_["shifted"], 1)
            act.activation(rt[1][:], rt[0][:], ACT.Exp).then_inc(s_["exped"], 1)
            act.activation(keep["neg_a"][:].rearrange("p n k -> p k n"), chan[:, :, C_ALOG:], ACT.Exp).then_inc(s_["neg_a"], 1)

            def silu(ch):
                for kt in range(KT):
                    act.wait_ge(s_["taps"], KT * (TAPS * ch + HALO) + kt + 1)
                    apart(act, s_["act_at"])
                    act.activation(xnT[:, ds(ch, 1), kt, HALO:], conv[:, kt, :].unsqueeze(1), ACT.Silu).then_inc(s_["silu"], 1)

            def copy_projection(ch):
                act.wait_ge(s_["proj"], ch + 2)
                act.wait_ge(s_["dt"], KT * ch + 1)
                act.activation(dtin[:], pX[:, 0, :], ACT.Copy).then_inc(s_["dtin"], 1)
                act.wait_ge(s_["bc_out"], 16 * ch + 16)
                act.activation(bcrows[:], pX[0:2 * N, 1, :], ACT.Copy).then_inc(s_["bc_rows"], 1)

            def softplus(ch):
                act.wait_ge(s_["soft"], 2 * ch + 2)
                for h in HALVES:
                    for kt in range(h.start, h.stop):
                        act.wait_ge(s_["dt"], KT * ch + kt + 2)
                        act.activation(z[:, kt, :], pT[:, kt, :], ACT.Identity, bias=chan[:, kt, C_DTB:C_DTB + 1]).then_inc(s_["dt_read"], 1)
                    act.wait_ge(s_["dt_read"], KT * ch + KT + h.stop)
                    act.activation(za[:, h], z[:, h], ACT.Abs).then_inc(s_["absz"], 1)
                    act.wait_ge(s_["absz"], 2 * ch + h.stop // 2)
                    act.activation(za[:, h], za[:, h], ACT.Exp, scale=-1.0).then_inc(s_["expz"], 1)
                act.wait_ge(s_["expz"], 2 * ch + 2)
                act.wait_ge(s_["delta_out"], 16 * ch + 16)
                act.wait_ge(s_["u_done"], 2 * ch + 1)
                for h in HALVES:
                    act.activation(ln[:, h], za[:, h], ACT.Ln, bias=1.0).then_inc(s_["lnz"], 1)

            def store_bc(ch):
                act.wait_ge(s_["bc_rows"], ch + 2)
                act.dma_start(dr.bc[ds(ch, 1)].rearrange("o n t -> n (o t)"), bcrows[:]).then_inc(s_["bc_out"], 16)

            silu(0)
            with act.Fori(0, NCH - 1) as ch:
                act.activation(warm[:], zeros[:, 0:1], ACT.Silu)
                copy_projection(ch)
                silu(ch + 1)
                store_bc(ch)
                softplus(ch)
            copy_projection(NCH - 1)
            store_bc(NCH - 1)
            softplus(NCH - 1)
            act.wait_ge(s_["bc_out"], 16 * NCH + 16)

        @block.gpsimd
        def _(pool):
            pool.sem_inc(s_["u_done"], 1)
            pool.wait_ge(s_["early"], 16 * len(early))

            def power(ch, i, u):
                pool.wait_ge(s_["moments"], ch + 1)
                apart(pool, s_["pool_at"])
                pool.tensor_copy(keep["mean"][:, ds(ch, 1), :], moments[:, u, :, 0].unsqueeze(1))
                pool.tensor_tensor(keep["rstd"][:, ds(ch, 1), :], moments[:, u, :, 1].unsqueeze(1), mhalf[:].unsqueeze(1), ALU.pow).then_inc(s_["power"], 1)

            over_pairs(pool, power)

            pool.wait_ge(s_["placed"], 1)
            pool.wait_ge(s_["defaults"], 16)
            choices = [(s, t) for s in range(2) for t in range(NT)]
            begin = 0
            for ch in range(NCH):
                end = min(len(choices), FIRST_SCATTERS + ch * NEXT_SCATTERS)
                for s, t in choices[begin:end]:
                    pool.indirect_dma_start(dr.slots, bass.IndirectOffsetOnAxis(ap=place[:, s, t:t + 1], axis=0),
                                            entry[:, s, t, :], None).then_inc(s_["scattered"], 16)
                begin = end
                pool.wait_ge(s_["rounded"], 2 * ch + 1)
                pool.tensor_tensor(back[:, HALVES[0]], za[:, HALVES[0]], back[:, HALVES[0]], ALU.subtract).then_inc(s_["dropped"], 1)
                pool.wait_ge(s_["u_out"], 32 * ch + 32)
                for n, h in enumerate(HALVES):
                    pool.wait_ge(s_["delta"], 2 * ch + n + 2)
                    pool.tensor_tensor(u_now[:, h], ln[:, h], xnT[:, ch, h, HALO:], ALU.mult).then_inc(s_["u_done"], 1)

        @block.vector
        def _(dve):
            dve.sem_inc(s_["normed"], 2)
            dve.sem_inc(s_["soft"], 2)
            dve.sem_inc(s_["delta"], 1)
            dve.memset(zeros[:], 0.0).then_inc(s_["cleared"], 1)

            def measure(ch, u, i):
                dve.wait_ge(s_[f"x_in{u}"], 16 * i + 16)
                for j in range(TPC):
                    dve.bn_stats(stats[:, j, :], xin[:, u, j, :]).then_inc(s_["stats"], 1)
                dve.wait_ge(s_["stats"], (TPC + 2) * ch + TPC)
                apart(dve, s_["dve_at"])
                for j in range(TPC):
                    op = dve.bn_aggr(moments[:, u, j, :], stats[:, j, :])
                op.then_inc(s_["stats"], 1)
                dve.wait_ge(s_["stats"], (TPC + 2) * ch + TPC + 1)
                dve.tensor_scalar(moments[:, u, :, 1], moments[:, u, :, 1], EPS, None, ALU.add).then_inc(s_["stats"], 1)
                dve.wait_ge(s_["stats"], (TPC + 2) * ch + TPC + 2)
                dve.sem_inc(s_["moments"], 1)

            def norm(ch, u, i):
                dve.wait_ge(s_["power"], ch + 1)
                dve.wait_ge(s_[f"xn_out{u}"], 16 * i + 16)
                dve.wait_ge(s_["xT"], KT * ch + 1)
                for j in range(TPC):
                    op = dve.tensor_scalar(xn[:, u, j, :], xin[:, u, j, :], moments[:, u, j, 0:1], keep["rstd"][:].rearrange("p c j -> p (c j)")[:, ds(TPC * ch + j, 1)],
                                           ALU.subtract, ALU.mult)
                op.then_inc(s_["normed"], 1)

            def normalise(ch, i, u):
                measure(ch, u, i)
                norm(ch, u, i)

            over_pairs(dve, normalise)

            dve.wait_ge(s_["consts"], 16 * len(consts))
            dve.wait_ge(s_["xT_copied"], KT * NCH + KT)
            for b in range(B):
                op = dve.memset(xnT[:, b * CPB, :, 0:HALO], 0.0)
            op.then_inc(s_["halo"], 1)

            def convolve(ch):
                dve.wait_ge(s_["silu"], KT * ch + 1)
                for k in range(TAPS):
                    for kt in range(KT):
                        x = xnT[:, ds(ch, 1), kt, HALO - k:HALO - k + CH]
                        c = conv[:, kt, :].unsqueeze(1)
                        tap = chan[:, kt, C_TAP + HALO - k:C_TAP + HALO - k + 1]
                        if k == 0:
                            op = dve.tensor_scalar(c, x, tap, chan[:, kt, C_CONVB:C_CONVB + 1], ALU.mult, ALU.add)
                        else:
                            dve.wait_ge(s_["taps"], KT * (TAPS * ch + k - 1) + kt + 1)
                            op = dve.scalar_tensor_tensor(out=c, in0=x, scalar=tap, in1=c, op0=ALU.mult, op1=ALU.add)
                        op.then_inc(s_["taps"], 1)
            dve.wait_ge(s_["halo"], 1)
            convolve(0)
            chain = [0]

            def link(op):
                chain[0] += 1
                op.then_inc(s_["route"], 1)
                dve.wait_ge(s_["route"], chain[0])

            def wide(x):
                return x[:].unsqueeze(2).to_broadcast([P, NT, E])

            dve.wait_ge(s_["lg_copied"], NCH + 1)
            link(dve.tensor_reduce(c0[:], logits[:], AX, ALU.max))
            dve.tensor_tensor(rt[0][:], logits[:], wide(c0), ALU.subtract).then_inc(s_["shifted"], 1)
            dve.wait_ge(s_["exped"], 1)
            link(dve.tensor_reduce(c1[:], rt[1][:], AX, ALU.add))
            link(dve.reciprocal(c2[:], c1[:]))
            link(dve.tensor_tensor(rt[2][:], rt[1][:], wide(c2), ALU.mult))
            score = rt[2]
            for s in range(2):
                link(dve.tensor_reduce(best[s][:], score[:], AX, ALU.max))
                link(dve.tensor_tensor(rt[0][:], score[:], wide(best[s]), ALU.is_equal))
                link(dve.tensor_tensor(rt[0][:], rt[0][:], rev[:], ALU.mult))
                link(dve.tensor_reduce(pick[s][:], rt[0][:], AX, ALU.max))
                link(dve.tensor_tensor(mask[s][:], rev[:], wide(pick[s]), ALU.is_equal))
                if s == 0:
                    score = rt[3]
                    link(dve.scalar_tensor_tensor(out=score[:], in0=mask[0][:], scalar=-2.0, in1=rt[2][:], op0=ALU.mult, op1=ALU.add))
            dve.sem_inc(s_["masks"], 1)
            link(dve.tensor_tensor(c0[:], best[0][:], best[1][:], ALU.add))
            link(dve.tensor_scalar(c0[:], c0[:], 1e-9, None, ALU.max))
            link(dve.reciprocal(c1[:], c0[:]))
            for s in range(2):
                link(dve.tensor_tensor(entry[:, s, :, 1], best[s][:], c1[:], ALU.mult))
                link(dve.tensor_copy(entry[:, s, :, 0], tokens[:, 0, :]))
            dve.wait_ge(s_["counted"], 1)
            for s in range(2):
                link(dve.tensor_copy(tot[:], pC[:, s, NT * E:].rearrange("p (t e) -> p e t", e=E)))
                link(dve.tensor_tensor_scan(incl[s][:].rearrange("p e t -> p (e t)"), reset[:].rearrange("p e t -> p (e t)"),
                                            tot[:].rearrange("p e t -> p (e t)"), 0.0, ALU.mult, ALU.add))
                link(dve.tensor_tensor(excl[:], incl[s][:], tot[:], ALU.subtract))
                if s == 1:
                    link(dve.tensor_tensor(excl[:], excl[:], incl[0][:, :, NT - 1:NT].to_broadcast([P, E, NT]), ALU.add))
                link(dve.tensor_tensor(rt[0][:], pC[:, s, 0:NT * E].rearrange("p (t e) -> p t e", e=E), excl[:].rearrange("p e t -> p t e"), ALU.add))
                link(dve.tensor_tensor(rt[0][:], rt[0][:], mask[s][:], ALU.mult))
                link(dve.tensor_reduce(c0[:], rt[0][:], AX, ALU.add))
                link(dve.tensor_scalar(c1[:], pick[s][:], -float(CAP), float(E * CAP - 1), ALU.mult, ALU.add))
                link(dve.tensor_tensor(c1[:], c1[:], c0[:], ALU.add))
                link(dve.tensor_scalar(c2[:], c0[:], float(CAP), None, ALU.is_le))
                link(dve.tensor_tensor(c1[:], c1[:], tokens[:, 1 + s, :], ALU.subtract))
                link(dve.tensor_tensor(c1[:], c1[:], c2[:], ALU.mult))
                link(dve.tensor_tensor(c1[:], c1[:], tokens[:, 1 + s, :], ALU.add))
                link(dve.tensor_copy(place[:, s, :], c1[:]))
            dve.sem_inc(s_["placed"], 1)
            dve.wait_ge(s_["neg_a"], 1)
            link(dve.tensor_scalar(keep["neg_a"][:], keep["neg_a"][:], -1.0, None, ALU.mult))

            def soft(ch):
                for n, h in enumerate(HALVES):
                    dve.wait_ge(s_["expz"], 2 * ch + n + 1)
                    dve.wait_ge(s_["delta"], 2 * ch + 1)
                    dve.tensor_scalar(back[:, h], za[:, h], 1.0, -1.0, ALU.add, ALU.add).then_inc(s_["rounded"], 1)
                h = HALVES[1]
                dve.wait_ge(s_["rounded"], 2 * ch + 2)
                dve.tensor_tensor(back[:, h], za[:, h], back[:, h], ALU.subtract).then_inc(s_["dropped_dve"], 1)
                for h in HALVES[::-1]:
                    dve.wait_ge(s_["dropped" if h.start == 0 else "dropped_dve"], ch + 1)
                    dve.scalar_tensor_tensor(out=back[:, h], in0=z[:, h], scalar=0.0, in1=back[:, h], op0=ALU.max, op1=ALU.add).then_inc(s_["soft"], 1)
                dve.wait_ge(s_["soft"], 2 * ch + 4)
                for n, h in enumerate(HALVES):
                    dve.wait_ge(s_["lnz"], 2 * ch + n + 1)
                    dve.tensor_tensor(ln[:, h], ln[:, h], back[:, h], ALU.add).then_inc(s_["delta"], 1)

            for ch in range(1, AHEAD):
                convolve(ch)
            with dve.Fori(0, NCH - AHEAD) as ch:
                convolve(ch + AHEAD)
                soft(ch)
            for ch in range(NCH - AHEAD, NCH - 1):
                soft(ch)
            dve.wait_ge(s_["table"], 16)
            dve.tensor_copy(keep["add_row"][:, 0], vacant[:, 0, :, 0])
            dve.tensor_copy(keep["add_row"][:, 1:], filled[:, :, :, 0])
            dve.tensor_copy(keep["gate"][:], filled[:, :, :, 1])
            dve.tensor_scalar(keep["row"][:, E], vacant[:, 0, :, 0], float(S - 1), None, ALU.min)
            dve.tensor_scalar(keep["row"][:, 0:E], filled[:, :, :, 0], float(S - 1), None, ALU.min).then_inc(s_["indexed"], 1)
            soft(NCH - 1)
            dve.wait_ge(s_["indexed"], 1)


def main_loop(nc, a, dr, keep):
    with ExitStack() as ctx:
        sb, psum, sems = memory(nc, ctx)
        ident = sb("m_ident", [P, P])
        raw = sb("w_raw", [P, KT * QH])
        w1h, w1l = sb("w1h", [P, KT, QH], F32R), sb("w1l", [P, KT, QH], F32R)
        w2h, w2l = sb("w2h", [P, HT, D], F32R), sb("w2l", [P, HT, D], F32R)
        xTh, xTl = sb("xTh", [P, KT, CAP], F32R), sb("xTl", [P, KT, CAP], F32R)
        hh, hl = sb("hh", [P, 2, HT, 512], F32R), sb("hl", [P, 2, HT, 512], F32R)
        part = sb("part", [P, TILES, D])
        b2 = sb("b2_sb", [P, D])
        got = sb("got", [P, 4, D])
        row_now = sb("row_now", [P, TILES], I32)
        add_now = sb("add_now", [P, TILES], I32)
        u, delta, s_acc = sb("u_sb", [P, KT, CH]), sb("delta_sb", [P, KT, CH]), sb("s_acc", [P, KT, CH])
        abuf = sb("a_sb", [P, 8, 2, CH])
        bbuf = sb("b_sb", [P, 2, 2, CH])
        bc = sb("bc_sb", [P, 2, 2, CH])
        state = sb("state", [P, N, KT])
        warm = sb("warm", [P, 2])
        ph = psum("ph", [P, 4, 512])
        pacc = psum("pacc", [P, 3, D])
        ptr = psum("ptr", [P, 512])
        s_ = sems("m_", """ident raw_in w_hi w_lo x_got0 x_got1 x_got2 x_got3 x_turned x_hi x_lo l1 gelu h_free l2
            acc_free exp a_free bmul scan carried product pool_product kept bc_in0 bc_in1 d_in u_in0 u_in1 s_out
            b2_in staged add_staged added0 added1 cleared biased pe_at act_at dve_at pool_at""")
        block = ctx.enter_context(nc.Block())
        NH = 8 * NQ
        ON_POOL = (3, 7)
        PC = NH - len(ON_POOL) * NQ + 1
        PQ = 8 - len(ON_POOL)
        GC, GQ = NH - PC, len(ON_POOL)

        def on_pool(i, last):
            return i in ON_POOL and not (last and i == 7)

        def products(e, q, i):
            return PC * e + PQ * q + i + 1 - sum(g < i for g in ON_POOL)

        def pool_products(e, q, i):
            return GC * e + GQ * q + ON_POOL.index(i) + 1

        LATE = 7

        def chunks(eng, body):
            with eng.Fori(0, B) as b:
                with eng.Fori(0, CPB) as c:
                    body(b * CPB + c)

        def quarters(e, eng, quarter):
            quarter(e * NQ, 0, True, False)
            with eng.Fori(1, NQ - 1) as q:
                quarter(e * NQ + q, q, False, False)
            quarter(e * NQ + NQ - 1, NQ - 1, False, True)

        @block.sync
        def _(sp):
            sp.dma_start(ident[:], a["ident"]).then_inc(s_["ident"], 16)

            def chunk(e):
                def step_bc(q, k, first):
                    if k == 0:
                        sp.wait_ge(s_["product"], products(e - 1, NQ - 1, 5) + 4 if first else products(e, q - 1, 5) + 4)
                    elif k == 1 and first:
                        sp.wait_ge(s_["product"], PC * e + 4)
                    elif k == 1:
                        sp.wait_ge(s_["pool_product"], pool_products(e, q - 1, 7))
                    elif k == 2:
                        sp.wait_ge(s_["product"], products(e, q, 1) + 4)
                    else:
                        sp.wait_ge(s_["pool_product"], pool_products(e, q, 3))
                    n = q * 4 + k
                    src = dr.bc[ds(e, 1)].rearrange("o (w n) t -> n (o w) t", w=2)[ds(n, 1)]
                    sp.dma_start(bc[:, k % 2], src.to_broadcast([P, 2, CH])).then_inc(s_[f"bc_in{k % 2}"], 16)

                def weights(it, which):
                    sp.wait_ge(s_["w_lo"], 2 * it + which + 1)
                    sp.wait_ge(s_["w_hi"], 2 * it + which + 1)
                    src = a["w1" if which == 0 else "w2"][ds(it, 1)].rearrange("o p f -> p (o f)")
                    sp.dma_start(raw[:], src).then_inc(s_["raw_in"], 16)

                def load_u(h):
                    sp.wait_ge(s_["bmul"], NH * e + 1 + h)
                    sp.dma_start(u[:, 2 * h:2 * h + 2], dr.u[ds(e, 1), :, 2 * h:2 * h + 2, :].rearrange("o p k t -> p (o k) t")).then_inc(s_[f"u_in{h}"], 16)

                def quarter(it, q, first, last):
                    weights(it, 0)
                    if first:
                        sp.wait_ge(s_["exp"], NH * e + 1)
                        sp.dma_start(delta[:], dr.delta[ds(e, 1)].rearrange("o p k t -> p (o k) t")).then_inc(s_["d_in"], 16)
                        load_u(0)
                    step_bc(q, 0, first)
                    if first:
                        load_u(1)
                        sp.wait_ge(s_["biased"], TILES * e + 1)
                        sp.dma_start(b2[:], a["fc2_b"][ds(e, 1)].to_broadcast([P, D])).then_inc(s_["b2_in"], 16)
                    weights(it, 1)
                    for k in range(1, 4):
                        step_bc(q, k, first)

                quarters(e, sp, quarter)

            chunks(sp, chunk)

        @block.tensor
        def _(pe):
            for name, credits in (("x_turned", 4), ("l1", 1), ("l2", 1)):
                pe.sem_inc(s_[name], credits)
            pe.wait_ge(s_["ident"], 16)

            def three(out, stat, mov, start, stop):
                (sh, sl), (mh, ml) = stat, mov
                pe.matmul(out, sl, mh, start=start, stop=False)
                pe.matmul(out, sh, ml, start=False, stop=False)
                return pe.matmul(out, sh, mh, start=False, stop=stop)

            def turn(e, t, bank):
                pe.wait_ge(s_[f"x_got{t % 4}"], 16 * (2 * e + t // 4) + 16)
                for kt in range(KT):
                    mm = pe.transpose(bank[:, kt * P:(kt + 1) * P], got[:, t % 4, kt * P:(kt + 1) * P], ident[:])
                mm.then_inc(s_["x_turned"], 1)

            for t in range(TILES):
                if t >= 4:
                    pe.wait_ge(s_["x_lo"], t - 4 + 3)
                turn(0, t, ph[:, t % 4, :])
            pe.wait_ge(s_["x_lo"], TILES + 2)

            def chunk(e):
                def quarter(it, q, first, last):
                    pe.wait_ge(s_["w_lo"], 2 * it + 2)
                    for g in range(2):
                        if first:
                            pe.wait_ge(s_["x_lo"], TILES * e + 4 * g + 6)
                        for j in range(HT):
                            pe.wait_ge(s_["h_free"], 8 * it + 4 * g + j + 1)
                            for kt in range(KT):
                                w = (w1h[:, kt, j * P:(j + 1) * P], w1l[:, kt, j * P:(j + 1) * P])
                                x = (xTh[:, kt, g * 512:(g + 1) * 512], xTl[:, kt, g * 512:(g + 1) * 512])
                                mm = three(ph[:, j, :], w, x, kt == 0, kt == KT - 1)
                            mm.then_inc(s_["l1"], 1)
                    pe.wait_ge(s_["w_lo"], 2 * it + 3)
                    for t in range(TILES):
                        g, c = t // 4, (t % 4) * P
                        pe.wait_ge(s_["h_free"], 8 * it + 4 * g + 8)
                        if t != 2:
                            pe.wait_ge(s_["acc_free"], 8 * it + (t if t > 2 else t + 1))
                        for j in range(HT):
                            mm = three(pacc[:, t % 3, :], (hh[:, g, j, c:c + P], hl[:, g, j, c:c + P]),
                                       (w2h[:, j, :], w2l[:, j, :]), j == 0, j == HT - 1)
                        mm.then_inc(s_["l2"], 1)
                        if last:
                            pe.wait_ge(s_["x_lo"], TILES * (e + 1) + t + 2)
                            turn(e + 1, t, ptr[:])

                quarters(e, pe, quarter)

            chunks(pe, chunk)

        @block.scalar
        def _(act):
            act.sem_inc(s_["w_hi"], 1)
            act.sem_inc(s_["exp"], 1)
            act.wait_ge(s_["cleared"], 1)

            def split_x(e, t, bank):
                act.wait_ge(s_["x_turned"], TILES * e + t + 5)
                act.activation(xTh[:, :, t * P:(t + 1) * P], bank.rearrange("p (k s) -> p k s", k=KT), ACT.Copy).then_inc(s_["x_hi"], 1)

            def split_w(it, which):
                hi = w1h if which == 0 else w2h
                act.wait_ge(s_["raw_in"], 16 * (2 * it + which) + 16)
                act.wait_ge(s_["l1" if which == 0 else "l2"], 8 * it + 1)
                act.activation(hi[:].rearrange("p k f -> p (k f)"), raw[:], ACT.Copy).then_inc(s_["w_hi"], 1)

            def chunk(e):
                def quarter(it, q, first, last):
                    def exp(i):
                        act.wait_ge(s_["a_free"], 8 * it + i + 1)
                        for k in range(2):
                            kt = 2 * (i % 2) + k
                            col = q * 16 + (i // 2) * 4 + kt
                            op = act.activation(abuf[:, i, k, :], delta[:, kt, :], ACT.Exp,
                                                scale=keep["neg_a"][:].rearrange("p n k -> p (n k)")[:, ds(col, 1)])
                        op.then_inc(s_["exp"], 1)

                    tokens = first and not isinstance(e, int)
                    lag = 3 if tokens else 0
                    for i in range(LATE + lag):
                        if tokens and i < TILES:
                            split_x(e, i, ptr[:])
                        if first and i == lag:
                            act.wait_ge(s_["d_in"], 16 * e + 16)
                        if i >= lag:
                            exp(i - lag)
                        if i == 3 and not (first and isinstance(e, int)):
                            split_w(it, 0)
                    act.activation(warm[:, 1:2], warm[:, 0:1], ACT.Gelu)
                    for g in range(2):
                        for j in range(HT):
                            act.wait_ge(s_["l1"], 8 * it + 4 * g + j + 2)
                            apart(act, s_["act_at"])
                            bias = keep["b1"][:, ds(4 * it + j, 1)]
                            act.activation(hh[:, g, j, :], ph[:, j, :], ACT.Gelu, bias=bias)
                            act.activation(ph[:, j, :], ph[:, j, :], ACT.Gelu, bias=bias).then_inc(s_["gelu"], 1)
                            if g == 0 and j == 1:
                                split_w(it, 1)
                        if g == 0:
                            for i in range(LATE, 8):
                                exp(i)

                quarters(e, act, quarter)

            for t in range(TILES):
                split_x(0, t, ph[:, t % 4, :])
                if t == 3:
                    split_w(0, 0)
            chunk(0)
            with act.Fori(1, NCH) as e:
                chunk(e)
            for t in range(TILES):
                split_x(NCH, t, ptr[:])

        @block.gpsimd
        def _(pool):
            pool.sem_inc(s_["w_lo"], 1)
            pool.sem_inc(s_["bmul"], 2)

            def stage_rows(e):
                pool.wait_ge(s_["x_turned"], TILES * e + 4)
                pool.tensor_copy(row_now[:], keep["row"][:, ds(e, 1), :].rearrange("p o j -> p (o j)")).then_inc(s_["staged"], 1)

            def gather(e, t):
                pool.wait_ge(s_["staged"], e + 1)
                pool.wait_ge(s_["x_turned"], TILES * e + t + 1)
                apart(pool, s_["pool_at"])
                pool.indirect_dma_start(got[:, t % 4, :], None, dr.xn, bass.IndirectOffsetOnAxis(ap=row_now[:, t:t + 1], axis=0)).then_inc(s_[f"x_got{t % 4}"], 16)

            def store_sum(e):
                for h in range(2):
                    pool.wait_ge(s_["a_free"], NH * e + 7 + h)
                    apart(pool, s_["pool_at"])
                    pool.dma_start(dr.s[ds(e, 1), :, 2 * h:2 * h + 2, :].rearrange("o p k t -> p (o k) t"),
                                   s_acc[:, 2 * h:2 * h + 2, :]).then_inc(s_["s_out"], 16)

            def stage_adds(e):
                pool.wait_ge(s_["acc_free"], 8 * NQ * e + 2)
                pool.tensor_copy(add_now[:], keep["add_row"][:, ds(e, 1), :].rearrange("p o j -> p (o j)")).then_inc(s_["add_staged"], 1)
                pool.wait_ge(s_["add_staged"], e + 1)
                apart(pool, s_["pool_at"])

            def add_tile(t):
                pool.indirect_dma_start(dr.y, bass.IndirectOffsetOnAxis(ap=add_now[:, t:t + 1], axis=0), part[:, t, :], None,
                                        compute_op=ALU.add).then_inc(s_[f"added{t // 4}"], 16)

            ADDS = {1: (0, 1), 2: (2, 3), 3: (4,), 4: (5, 6), 5: (7,)}
            GATHERS = {1: (0, 1), 2: (2,), 3: (3,), 5: (4, 5), 6: (6,), 7: (7,)}

            stage_rows(0)
            for t in range(TILES):
                gather(0, t)

            def chunk(e):
                def quarter(it, q, first, last):
                    def low(which):
                        hi, lo = ((w1h, w1l), (w2h, w2l))[which]
                        pool.wait_ge(s_["w_hi"], 2 * it + which + 2)
                        pool.tensor_tensor(lo[:].rearrange("p k f -> p (k f)"), raw[:], hi[:].rearrange("p k f -> p (k f)").bitcast(F32), ALU.subtract).then_inc(s_["w_lo"], 1)

                    def multiply_c(it, i):
                        pool.wait_ge(s_["carried"], 8 * it + i + 1)
                        pool.tensor_tensor(abuf[:, i], abuf[:, i], bc[:, i // 2 % 2, 1:2, :].to_broadcast([P, 2, CH]), ALU.mult).then_inc(s_["pool_product"], 1)

                    low(0)
                    for i in range(8):
                        m = i // 2
                        if first and i < 2:
                            pool.wait_ge(s_[f"u_in{i}"], 16 * e + 16)
                        if i % 2 == 0:
                            pool.wait_ge(s_[f"bc_in{m % 2}"], 16 * (2 * it + m // 2) + 16)
                        pool.wait_ge(s_["scan"], 8 * it + i + 1)
                        h = 2 * (i % 2)
                        pool.tensor_tensor(bbuf[:, i % 2], u[:, h:h + 2, :], bc[:, m % 2, 0:1, :].to_broadcast([P, 2, CH]), ALU.mult).then_inc(s_["bmul"], 1)
                        if i == 2:
                            low(1)
                        if i == 0 and not first:
                            multiply_c(it - 1, 7)
                        if i > 0 and on_pool(i - 1, last):
                            multiply_c(it, i - 1)
                        if first:
                            if i == 1:
                                store_sum(e)
                                stage_adds(e)
                            for t in ADDS.get(i, ()):
                                add_tile(t)
                        if last:
                            if i == 0:
                                stage_rows(e + 1)
                            for t in GATHERS.get(i, ()):
                                gather(e + 1, t)

                quarters(e, pool, quarter)

            chunks(pool, chunk)
            pool.tensor_copy(add_now[:], keep["add_row"][:, NCH, :]).then_inc(s_["add_staged"], 1)
            pool.wait_ge(s_["add_staged"], NCH + 1)
            for t in range(TILES):
                pool.wait_ge(s_["acc_free"], 8 * NQ * NCH - 8 + t + 3)
                add_tile(t)
            store_sum(NCH)
            pool.wait_ge(s_["s_out"], 32 * (NCH + 1))
            for g in range(2):
                pool.wait_ge(s_[f"added{g}"], 64 * (NCH + 1))

        @block.vector
        def _(dve):
            dve.memset(warm[:], 0.0).then_inc(s_["cleared"], 1)
            dve.memset(part[:], 0.0).then_inc(s_["cleared"], 1)
            dve.memset(s_acc[:], 0.0).then_inc(s_["cleared"], 1)
            dve.wait_ge(s_["cleared"], 3)
            for name, credits in (("x_lo", 2), ("h_free", 4), ("acc_free", 2), ("a_free", 8), ("scan", 2),
                                  ("product", 4), ("biased", 1)):
                dve.sem_inc(s_[name], credits)
            def low_x(e, t, bank):
                dve.wait_ge(s_["x_hi"], TILES * e + t + 1)
                dve.tensor_tensor(xTl[:, :, t * P:(t + 1) * P], bank.rearrange("p (k s) -> p k s", k=KT),
                                  xTh[:, :, t * P:(t + 1) * P].bitcast(F32), ALU.subtract).then_inc(s_["x_lo"], 1)

            for t in range(TILES):
                low_x(0, t, ph[:, t % 4, :])

            def chunk(e):
                def low_h(it, s):
                    g, j = s // 4, s % 4
                    dve.wait_ge(s_["gelu"], 8 * it + s + 1)
                    dve.tensor_tensor(hl[:, g, j, :], ph[:, j, :], hh[:, g, j, :].bitcast(F32), ALU.subtract).then_inc(s_["h_free"], 1)

                def add_part(it, t, first):
                    gate = keep["gate"][:].rearrange("p e j -> p (e j)")[:, ds(8 * e + t, 1)]
                    if first:
                        if t % 4 == 0:
                            dve.wait_ge(s_[f"added{t // 4}"], 64 * e + 64)
                            dve.wait_ge(s_["b2_in"], 16 * e + 16)
                        dve.tensor_scalar(part[:, t, :], b2[:], gate, None, ALU.mult).then_inc(s_["biased"], 1)
                        dve.wait_ge(s_["biased"], TILES * e + t + 2)
                    dve.wait_ge(s_["l2"], 8 * it + t + 2)
                    dve.scalar_tensor_tensor(out=part[:, t, :], in0=pacc[:, t % 3, :], scalar=gate, in1=part[:, t, :],
                                             op0=ALU.mult, op1=ALU.add).then_inc(s_["acc_free"], 1)

                def sum_up(q, i, first, last):
                    if first and i < 2:
                        return
                    if on_pool(i, last):
                        dve.wait_ge(s_["pool_product"], pool_products(e, q, i))
                    else:
                        dve.wait_ge(s_["product"], products(e, q, i) + 4)
                    acc = s_acc[:, 2 * (i % 2):2 * (i % 2) + 2, :]
                    if first and i < 4:
                        if i == 2:
                            dve.wait_ge(s_["s_out"], 32 * e + 32)
                        dve.tensor_tensor(acc, abuf[:, i - 2], abuf[:, i], ALU.add).then_inc(s_["a_free"], 1 if i == 2 else 3)
                    else:
                        dve.tensor_tensor(acc, acc, abuf[:, i], ALU.add).then_inc(s_["a_free"], 1)

                def quarter(it, q, first, last):
                    st = state[:].rearrange("p n k -> p (n k)")

                    def carry(i):
                        dve.wait_ge(s_["scan"], 8 * it + i + 3)
                        apart(dve, s_["dve_at"])
                        col = q * 16 + (i // 2) * 4 + 2 * (i % 2)
                        dve.tensor_copy(st[:, ds(col, 2)].unsqueeze(2), abuf[:, i, :, CH - 1:CH]).then_inc(s_["carried"], 1)

                    for s in range(16):
                        i, hs = s // 2, 8 * it + s // 2
                        m, kt0 = i // 2, 2 * (i % 2)
                        if s % 2 == 0:
                            dve.wait_ge(s_["exp"], hs + 2)
                            dve.wait_ge(s_["bmul"], hs + 3)
                            for k in range(2):
                                col = q * 16 + m * 4 + kt0 + k
                                op = dve.tensor_tensor_scan(abuf[:, i, k, :], abuf[:, i, k, :], bbuf[:, i % 2, k, :],
                                                            st[:, ds(col, 1)], ALU.mult, ALU.add)
                            op.then_inc(s_["scan"], 1)
                            if on_pool(i, last):
                                carry(i)
                        if last and s >= 8:
                            low_x(e + 1, s - 8, ptr[:])
                        if s % 2 == 0:
                            if s >= 8:
                                add_part(it, s - 8, first)
                            if i > 0:
                                sum_up(q, i - 1, first, last)
                            elif not first:
                                sum_up(q - 1, 7, False, False)
                            if s < 8:
                                low_h(it, s)
                        else:
                            if not on_pool(i, last):
                                carry(i)
                            if s < 8:
                                low_h(it, s)
                            else:
                                add_part(it, s - 8, first)
                        if s % 2 == 1 and not on_pool(i, last):
                            dve.wait_ge(s_["carried"], hs + 1)
                            dve.tensor_tensor(abuf[:, i], abuf[:, i], bc[:, m % 2, 1:2, :].to_broadcast([P, 2, CH]), ALU.mult).then_inc(s_["product"], 1)
                    if last:
                        sum_up(q, 7, False, True)

                quarters(e, dve, quarter)

            with dve.Fori(0, B) as b:
                dve.memset(state[:], 0.0).then_inc(s_["kept"], 1)
                dve.wait_ge(s_["kept"], b + 1)
                apart(dve, s_["dve_at"])
                with dve.Fori(0, CPB) as c:
                    chunk(b * CPB + c)


def tail(nc, a, dr, keep, out):
    with ExitStack() as ctx:
        sb, psum, sems = memory(nc, ctx)
        TPP = 2
        RING = 4
        PC, NP = TPP * P, NT // TPP
        ident = sb("t_ident", [P, P])
        d_row = sb("t_D", [P, D])
        sT = sb("t_sT", [P, RING, KT, PC])
        y, x = sb("t_y", [P, RING, TPP, D]), sb("t_x", [P, RING, TPP, D])
        g, o = sb("t_g", [P, RING, TPP, D]), sb("t_o", [P, RING, TPP, D])
        ps = psum("t_s", [P, RING, TPP, D])
        rings = " ".join(f"in{u} out{u}" for u in range(RING))
        s_ = sems("t_", f"consts {rings} turned silu xn skip whole gated sum")
        block = ctx.enter_context(nc.Block())

        def over_rings(eng, body):
            with eng.Fori(0, NP // RING) as i:
                for u in range(RING):
                    body(RING * i + u, i, u)

        @block.sync
        def _(sp):
            for u in range(RING):
                sp.sem_inc(s_[f"out{u}"], 16)
            sp.dma_start(ident[:], a["ident"]).then_inc(s_["consts"], 16)
            sp.dma_start(d_row[:], a["D"].to_broadcast([P, D])).then_inc(s_["consts"], 16)

            def load(c, half, p, u):
                sp.wait_ge(s_["sum"], p + 1)
                sp.dma_start(x[:, u], a["x"][ds(c, 1), :, TPP * half:TPP * (half + 1), :].rearrange("o p j d -> p (o j) d")).then_inc(s_[f"in{u}"], 16)
                sp.dma_start(sT[:, u], dr.s[ds(c + 1, 1), :, :, PC * half:PC * (half + 1)].rearrange("o p k t -> p (o k) t")).then_inc(s_[f"in{u}"], 16)
                sp.dma_start(y[:, u], dr.y[ds(p * PC, PC)].rearrange("(j p) d -> p j d", p=P)).then_inc(s_[f"in{u}"], 16)

            def store(p, u):
                sp.wait_ge(s_["sum"], p + RING + 1)
                sp.dma_start(out[ds(p, 1)].rearrange("o (j p) d -> p (o j) d", p=P), o[:, u]).then_inc(s_[f"out{u}"], 16)

            for u in range(RING):
                load(u // 2, u % 2, u, u)
            with sp.Fori(1, NP // RING) as i:
                for u in range(RING):
                    store(RING * i + u - RING, u)
                    load(RING // 2 * i + u // 2, u % 2, RING * i + u, u)
            for u in range(RING):
                store(NP - RING + u, u)
            for u in range(RING):
                sp.wait_ge(s_[f"out{u}"], 16 * NP // RING + 16)

        @block.tensor
        def _(pe):
            pe.wait_ge(s_["consts"], 32)

            def turn(p, i, u):
                pe.wait_ge(s_[f"in{u}"], 48 * i + 48)
                pe.wait_ge(s_["whole"], p + 1)
                for j in range(TPP):
                    for kt in range(KT):
                        mm = pe.transpose(ps[:, u, j, kt * P:(kt + 1) * P], sT[:, u, kt, j * P:(j + 1) * P], ident[:])
                mm.then_inc(s_["turned"], 1)

            over_rings(pe, turn)

        @block.scalar
        def _(act):
            def silu(p, i, u):
                act.wait_ge(s_[f"in{u}"], 48 * i + 48)
                act.wait_ge(s_["gated"], p + 1)
                act.activation(g[:, u], y[:, u], ACT.Silu).then_inc(s_["silu"], 1)

            over_rings(act, silu)

        @block.gpsimd
        def _(pool):
            pool.wait_ge(s_["consts"], 32)

            def skip(p, i, u):
                pool.wait_ge(s_["xn"], p + 1)
                pool.tensor_tensor(o[:, u], o[:, u], d_row[:].unsqueeze(1).to_broadcast([P, TPP, D]), ALU.mult).then_inc(s_["skip"], 1)

            over_rings(pool, skip)

        @block.vector
        def _(dve):
            for name in ("whole", "gated", "sum"):
                dve.sem_inc(s_[name], RING)

            def normalise(p, i, u):
                dve.wait_ge(s_[f"in{u}"], 48 * i + 48)
                dve.wait_ge(s_[f"out{u}"], 16 * i + 16)
                for j in range(TPP):
                    mean, rstd = (keep[k][:].rearrange("p c j -> p (c j)")[:, ds(TPP * p + j, 1)] for k in ("mean", "rstd"))
                    op = dve.tensor_scalar(o[:, u, j, :], x[:, u, j, :], mean, rstd, ALU.subtract, ALU.mult)
                op.then_inc(s_["xn"], 1)

            def combine(p, u):
                dve.wait_ge(s_["skip"], p + 1)
                dve.wait_ge(s_["turned"], p + 1)
                dve.tensor_tensor(o[:, u], o[:, u], ps[:, u], ALU.add).then_inc(s_["whole"], 1)
                dve.wait_ge(s_["whole"], p + RING + 1)
                dve.wait_ge(s_["silu"], p + 1)
                dve.tensor_tensor(o[:, u], o[:, u], g[:, u], ALU.mult).then_inc(s_["gated"], 1)
                dve.wait_ge(s_["gated"], p + RING + 1)
                dve.tensor_tensor(o[:, u], o[:, u], x[:, u], ALU.add).then_inc(s_["sum"], 1)

            normalise(0, 0, 0)
            with dve.Fori(0, NP // RING - 1) as i:
                for u in range(RING):
                    normalise(RING * i + u + 1, i + (u + 1) // RING, (u + 1) % RING)
                    combine(RING * i + u, u)
            for u in range(RING):
                if u < RING - 1:
                    normalise(NP - RING + u + 1, NP // RING - 1, u + 1)
                combine(NP - RING + u, u)


def build(nc, a, out):
    dr = Scratch(nc)
    with ExitStack() as ctx:
        sb, _, _ = memory(nc, ctx)
        keep = {
            "mean": sb("mean_keep", [P, NCH, TPC]),
            "rstd": sb("rstd_keep", [P, NCH, TPC]),
            "b1": sb("b1_keep", [P, E * HID // P]),
            "neg_a": sb("neg_a_keep", [P, N, KT]),
            "row": sb("row_keep", [P, E + 1, TILES], I32),
            "add_row": sb("add_row_keep", [P, E + 1, TILES], I32),
            "gate": sb("gate_keep", [P, E, TILES]),
        }
        front(nc, a, dr, keep)
        main_loop(nc, a, dr, keep)
        tail(nc, a, dr, keep, out)


def lay_out(i):
    def per_channel(x):
        return x.reshape(KT, P, -1).transpose(1, 0, 2)

    chan = np.concatenate([per_channel(x) for x in (
        i["L0_attn_conv_w"].reshape(D, TAPS), i["L0_attn_conv_b"], i["L0_attn_dtproj_b"], i["L0_attn_A_log"])], axis=2)
    w1 = i["L0_ffn_fc1_w"].reshape(E, KT, P, NQ, QH).transpose(0, 3, 2, 1, 4)
    w2 = i["L0_ffn_fc2_w"].reshape(E, NQ, HT, P, D).transpose(0, 1, 3, 2, 4)
    return {
        "x": i["L0_attn_x"].reshape(NCH, TPC, P, D).transpose(0, 2, 1, 3),
        "chan": chan,
        "D": i["L0_attn_D_param"].reshape(1, D),
        "xprojT": i["L0_attn_xproj_w"].T.reshape(KT, P, R + 2 * N).transpose(1, 0, 2),
        "dtprojT": i["L0_attn_dtproj_w"].T,
        "wg": i["L0_ffn_wg"].reshape(KT, P, E).transpose(1, 0, 2),
        "w1": w1.reshape(E * NQ, P, KT * QH),
        "w2": w2.reshape(E * NQ, P, HT * D),
        "fc1_b": i["L0_ffn_fc1_b"].reshape(E * HID // P, P).T,
        "fc2_b": i["L0_ffn_fc2_b"],
    }


def constants():
    f = np.float32
    token = (np.arange(NT)[None, :] * P + np.arange(P)[:, None]).astype(f)
    slot = np.arange(CAP).reshape(P, TILES)
    vacant = np.zeros((P, E, TILES, 2), f)
    vacant[..., 0] = (S + slot)[:, None, :]
    reset = np.ones((P, E, NT), f)
    reset[:, :, 0] = 0
    return {
        "ident": np.eye(P, dtype=f),
        "tri": np.triu(np.ones((P, P), f)),
        "ones": np.ones((P, P), f),
        "rev": np.broadcast_to((E - np.arange(E)).astype(f), (P, NT, E)),
        "reset": reset,
        "tokens": np.stack([token, TRASH + token, TRASH + S + token], axis=1),
        "mhalf": np.full((P, TPC), -0.5, f),
        "vacant": vacant,
    }


def kernel(**inputs):
    import concourse.bacc as bacc
    from concourse.bass_utils import run_bass_kernel_spmd

    nc = bacc.Bacc("TRN2", target_bir_lowering=False, num_devices=1)
    given = lay_out({k: np.asarray(v) for k, v in inputs.items()})
    given.update(constants())
    arrays, aps = {}, {}
    for name, value in given.items():
        value = np.ascontiguousarray(value)
        arrays[f"in_{name}"] = value
        aps[name] = nc.dram_tensor(f"in_{name}", value.shape, mybir.dt.from_np(value.dtype), kind="ExternalInput").ap()
    out = nc.dram_tensor("out", (NT // 2, 2 * P, D), F32, kind="ExternalOutput").ap()
    build(nc, aps, out)
    r = run_bass_kernel_spmd(nc, [arrays], core_ids=[0])
    return np.asarray(r.results[0]["out"]).reshape(B, T, D)
```
